# Optimizing a Trainium2 kernel written in Bass

```python
import numpy as np
import jax
import jax.numpy as jnp

def _softmax(x, axis=-1):
    return jax.nn.softmax(x, axis=axis)

def _gelu(x):
    return jax.nn.gelu(x, approximate=True)

def _silu(x):
    return jax.nn.silu(x)

def _sigmoid(x):
    return jax.nn.sigmoid(x)

def _layernorm(x, axis=-1, eps=1e-05):
    m = jnp.mean(x, axis=axis, keepdims=True)
    v = jnp.var(x, axis=axis, keepdims=True)
    return (x - m) / jnp.sqrt(v + eps)

def _scatter_add(tgt, idx, src, axis=0):
    return tgt.at[idx].add(src)

def _segment_sum(src, seg, n):
    return jax.ops.segment_sum(src, seg, n)
kernel_name = 'mk_xattn_ffn_d1_seqx_r8_d9a661'

def setup_inputs(seed: int=0):
    np.random.seed(seed)
    _w = jnp.asarray

    def _rec_inputs():
        import jax
        import jax.numpy as jnp
        _rk = jax.random.key(seed)
        x = -0.0002928 + 1 * jax.random.normal(jax.random.fold_in(_rk, 1), (2, 512, 128), jnp.float32)
        _lenS = 512 - jax.random.randint(jax.random.fold_in(_rk, 7), (2,), 0, max(1, 512 // 4) + 1, jnp.int32)
        _lenS2 = 32 - jax.random.randint(jax.random.fold_in(_rk, 8), (2,), 0, max(1, 32 // 4) + 1, jnp.int32)
        _ctx_1024P = jax.random.normal(jax.random.fold_in(_rk, 11), (2, 16, 128), jnp.float32)
        _ctx_1024c = jax.random.dirichlet(jax.random.fold_in(_rk, 511), 0.3 * jnp.ones((16,), jnp.float32), (2, 32))
        _ctx_1024t = jnp.einsum('bsk,bkd->bsd', _ctx_1024c, _ctx_1024P)
        _ctx_1024t = _ctx_1024t * jax.lax.rsqrt(jnp.mean(jnp.square(_ctx_1024t)) + 1e-12) * 0.953939
        ctx_1024 = -0.000292821 + 1.00034 * (_ctx_1024t + 0.3 * jax.random.normal(jax.random.fold_in(_rk, 611), (2, 32, 128), jnp.float32))
        return (x, ctx_1024)
    x, ctx_1024 = _rec_inputs()

    def _L0_xattn_setup():
        import jax, jax.numpy as jnp
        import numpy as np
        HIDDEN = 128
        HEADS = 16
        HEAD_DIM = HIDDEN // HEADS
        SCALE = 1.0 / np.sqrt(HEAD_DIM).astype(np.float32)
        key = jax.random.key(seed)
        ks = jax.random.split(key, 8)
        b, t = (2, 256)
        x = jax.random.normal(ks[0], (b, t, HIDDEN), dtype=jnp.float32)
        context = x
        s = 0.02
        Wq = jax.random.normal(ks[1], (HIDDEN, HIDDEN), dtype=jnp.float32) * s
        Wk = jax.random.normal(ks[2], (HIDDEN, HIDDEN), dtype=jnp.float32) * s
        Wv = jax.random.normal(ks[3], (HIDDEN, HIDDEN), dtype=jnp.float32) * s
        Wo = jax.random.normal(ks[4], (HIDDEN, HIDDEN), dtype=jnp.float32) * s
        bo = jnp.zeros((HIDDEN,), dtype=jnp.float32)
        return {'x': x, 'context': context, 'Wq': Wq, 'Wk': Wk, 'Wv': Wv, 'Wo': Wo, 'bo': bo}
    _L0_xattn_all = _L0_xattn_setup()
    _L0_xattn_in = {k: v for k, v in _L0_xattn_all.items() if k in ('Wq', 'Wk', 'Wv', 'Wo', 'bo')}
    del _L0_xattn_all

    def _L0_ffn_setup():
        import jax, jax.numpy as jnp
        import numpy as np
        B, S, D, F, E = (1, 128, 128, 512, 8)
        EPS = 1e-05

        def _sublayer(xs, g, b, W1e, b1e, W2e, b2e):
            mu = jnp.mean(xs, axis=-1, keepdims=True)
            var = jnp.mean(jnp.square(xs - mu), axis=-1, keepdims=True)
            h = (xs - mu) * jax.lax.rsqrt(var + EPS) * g + b
            return xs + jax.nn.relu(h @ W1e.T + b1e) @ W2e.T + b2e
        key = jax.random.key(seed)
        ks = jax.random.split(key, 4)
        x = jax.random.normal(ks[0], (B, S, D), jnp.float32)
        centroids = jax.random.normal(ks[1], (E, D), jnp.float32) * 0.1
        gamma = jnp.ones((E, D), jnp.float32)
        beta = jnp.zeros((E, D), jnp.float32)
        W1 = jax.random.normal(ks[2], (E, F, D), jnp.float32) * 0.02
        b1 = jnp.zeros((E, F), jnp.float32)
        W2 = jax.random.normal(ks[3], (E, D, F), jnp.float32) * 0.02
        b2 = jnp.zeros((E, D), jnp.float32)
        return {'x': x, 'centroids': centroids, 'gamma': gamma, 'beta': beta, 'W1': W1, 'b1': b1, 'W2': W2, 'b2': b2}
    _L0_ffn_all = _L0_ffn_setup()
    _L0_ffn_in = {k: v for k, v in _L0_ffn_all.items() if k in ('centroids', 'gamma', 'beta', 'W1', 'b1', 'W2', 'b2')}
    del _L0_ffn_all
    return {'x': x, 'ctx_1024': ctx_1024, 'L0_xattn_Wq': _L0_xattn_in['Wq'], 'L0_xattn_Wk': _L0_xattn_in['Wk'], 'L0_xattn_Wv': _L0_xattn_in['Wv'], 'L0_xattn_Wo': _L0_xattn_in['Wo'], 'L0_xattn_bo': _L0_xattn_in['bo'], 'L0_ffn_centroids': _L0_ffn_in['centroids'], 'L0_ffn_gamma': _L0_ffn_in['gamma'], 'L0_ffn_beta': _L0_ffn_in['beta'], 'L0_ffn_W1': _L0_ffn_in['W1'], 'L0_ffn_b1': _L0_ffn_in['b1'], 'L0_ffn_W2': _L0_ffn_in['W2'], 'L0_ffn_b2': _L0_ffn_in['b2']}

def reference(x, ctx_1024, L0_xattn_Wq, L0_xattn_Wk, L0_xattn_Wv, L0_xattn_Wo, L0_xattn_bo, L0_ffn_centroids, L0_ffn_gamma, L0_ffn_beta, L0_ffn_W1, L0_ffn_b1, L0_ffn_W2, L0_ffn_b2):
    import jax
    import jax.numpy as jnp

    def _L0_xattn_ref(x, context, Wq, Wk, Wv, Wo, bo):
        import jax, jax.numpy as jnp
        import numpy as np
        HIDDEN = 128
        HEADS = 16
        HEAD_DIM = HIDDEN // HEADS
        SCALE = 1.0 / np.sqrt(HEAD_DIM).astype(np.float32)
        b, t, c = x.shape
        kv_t = context.shape[1]
        q = x @ Wq.T
        k = context @ Wk.T
        v = context @ Wv.T
        q = q.reshape(b, t, HEADS, HEAD_DIM).transpose(0, 2, 1, 3)
        k = k.reshape(b, kv_t, HEADS, HEAD_DIM).transpose(0, 2, 1, 3)
        v = v.reshape(b, kv_t, HEADS, HEAD_DIM).transpose(0, 2, 1, 3)
        scores = jnp.einsum('bhqd,bhkd->bhqk', q, k) * SCALE
        causal = jnp.tril(jnp.ones((t, kv_t), dtype=bool))
        scores = jnp.where(causal[None, None, :, :], scores, -jnp.inf)
        probs = jax.nn.softmax(scores, axis=-1)
        y = jnp.einsum('bhqk,bhkd->bhqd', probs, v)
        y = y.transpose(0, 2, 1, 3).reshape(b, t, c)
        return y @ Wo.T + bo

    def _L0_ffn_ref(x, centroids, gamma, beta, W1, b1, W2, b2):
        import jax, jax.numpy as jnp
        import numpy as np
        B, S, D, F, E = (1, 128, 128, 512, 8)
        EPS = 1e-05

        def _sublayer(xs, g, b, W1e, b1e, W2e, b2e):
            mu = jnp.mean(xs, axis=-1, keepdims=True)
            var = jnp.mean(jnp.square(xs - mu), axis=-1, keepdims=True)
            h = (xs - mu) * jax.lax.rsqrt(var + EPS) * g + b
            return xs + jax.nn.relu(h @ W1e.T + b1e) @ W2e.T + b2e
        feats = x.reshape(-1, x.shape[-1])
        scores = jax.lax.stop_gradient(feats @ centroids.T)
        expert = jnp.argmax(scores, axis=1)
        onehot = jax.nn.one_hot(expert, E, dtype=feats.dtype)
        alpha = jax.nn.sigmoid(jnp.sum(feats * centroids[expert], axis=-1, keepdims=True))
        ys = jax.vmap(_sublayer, in_axes=(None, 0, 0, 0, 0, 0, 0))(feats, gamma, beta, W1, b1, W2, b2)
        y = jnp.einsum('te,etd->td', onehot, ys)
        out = alpha * y + (1.0 - alpha) * feats
        return out.reshape(x.shape)
    x = x + _L0_xattn_ref(_layernorm(x, axis=-1), ctx_1024, L0_xattn_Wq, L0_xattn_Wk, L0_xattn_Wv, L0_xattn_Wo, L0_xattn_bo)
    x = x + _L0_ffn_ref(_layernorm(x, axis=-1), L0_ffn_centroids, L0_ffn_gamma, L0_ffn_beta, L0_ffn_W1, L0_ffn_b1, L0_ffn_W2, L0_ffn_b2)
    return x

_drawn_inputs = setup_inputs


def setup_inputs(seed=0):
    import zlib

    import numpy as np

    out = dict(_drawn_inputs(seed))
    spreads = {'L0_xattn_bo': (0.0, 0.1),
     'L0_ffn_gamma': (1.0, 0.6),
     'L0_ffn_beta': (0.0, 2.0),
     'L0_ffn_b1': (0.0, 0.619),
     'L0_ffn_b2': (0.0, 0.1)}
    factors = {'L0_xattn_Wq': 8.0, 'L0_xattn_Wk': 8.0}
    for name, (base, spread) in spreads.items():
        noise = np.random.default_rng([zlib.crc32(name.encode()), seed]).standard_normal(out[name].shape)
        drawn = base * np.exp(spread * noise) if base else spread * noise
        out[name] = jnp.asarray(drawn.astype(out[name].dtype))
    for name, factor in factors.items():
        out[name] = (out[name] * factor).astype(out[name].dtype)
    return out
```

```python
from contextlib import ExitStack

import concourse.bass as bass
from concourse import mybir

F32 = mybir.dt.float32
BF16 = mybir.dt.bfloat16
I32 = mybir.dt.int32
ALU = mybir.AluOpType
ACT = mybir.ActivationFunctionType
X = mybir.AxisListType.X

P = 128
B, T, D = 2, 512, 128
TB = T // P
NT = B * TB
KV = 32
H, HD = 16, 8
HC = P // KV
C = H // HC
E, F = 8, 512
FC = F // P
EPS = 1e-5
SCALE = float(HD) ** -0.5
NEG = -1e37
NS = NT + E - 1
ROW = D + 4
LANES = 4
VW = HC * HD + HC
YW = D + E
NOBODY = 4096.0

PA = dict(wk=0, ctx=128, wv=192, wq=320)
PA_W = 448
PB = dict(wo=0, wot=128, cen=256, gam=264, bet=272, bo=280)
PB_W = 281
CF = dict(ident=0, gap=128, center=136, hmask=264, vmask=280, ones=312, desc=316, token=324, expert=332, slot=340)
CF_W = 356
CB = dict(ident=0, before=128, ones=256, spread=384, causal=896)
CB_W = 1024


def xattn_moe(nc, x, xt, pa, pb, cf, cb, b12, w1, w2, out):
    rows = nc.dram_tensor("dispatched", [NS * P, ROW], F32, kind="Internal").ap()
    out_rows = out.rearrange("b t d -> (b t) d")
    x_tiles = x.rearrange("b (t p) d -> b p t d", p=P)
    ctx = ExitStack()
    with ctx:
        def sb(name, shape, dt=F32):
            return ctx.enter_context(nc.sbuf_tensor(name, shape, dt))

        def sem(name):
            return ctx.enter_context(nc.semaphore(name))

        xs = sb("xs", [P, NT, D])
        xts = sb("xts", [P, NT * P])
        pas = sb("pas", [P, PA_W])
        pbs = sb("pbs", [P, PB_W])
        cfs = sb("cfs", [P, CF_W])
        cbw = sb("cbw", [P, CB_W], mybir.dt.uint16)
        cbs = cbw[:, :].bitcast(BF16)
        b12s = sb("b12s", [1, E * F + E * D])
        w1s = sb("w1s", [P, E, F])
        w2s = sb("w2s", [P, E, FC * D])
        b12b = sb("b12b", [P, E * F + E * D])
        b1b = b12b[:, 0:E * F].rearrange("p (e f) -> p e f", e=E)
        b2b = b12b[:, E * F:].rearrange("p (e d) -> p e d", e=E)
        ident = cfs[:, 0:P]
        identb = cbs[:, 0:P]
        identc = cfs[:, 0:YW]
        wo_ext = pbs[:, PB["wot"]:PB["wot"] + YW]
        desc = cfs[:, CF["desc"]:CF["desc"] + E]
        kblk = sb("kblk", [P, B, H, KV])
        ctx4 = sb("ctx4", [P, B, HC, KV])
        v4 = sb("v4", [P, B, C, VW])
        ms = sb("ms", [P, B, H * KV])
        st = sb("st", [P, NT, 6])
        mv = sb("mv", [P, NT, 2])
        ve = sb("ve", [P, NT])
        mhalf = sb("mhalf", [P, 2, NT])
        rs = sb("rs", [P, NT])
        xn = sb("xn", [P, NT, D])
        xnt = sb("xnt", [P, NT * P])
        nm = sb("nm", [P, B, TB, H])
        nm2 = sb("nm2", [P, B, TB, 2, H], BF16)
        nmt = sb("nmt", [2 * H, B, T], BF16)
        pt = sb("pt", [P, B, C, T])
        rden = sb("rden", [P, B, TB * C, HC])
        o = sb("o", [P, B, T])
        ot = sb("ot", [P, B, T])
        st2 = sb("st2", [P, NT, 6])
        mv2 = sb("mv2", [P, NT, 2])
        u2 = sb("u2", [P, B, 2, TB])
        r2 = sb("r2", [P, B, 2, TB])
        nmr = sb("nmr", [P, B, 3, TB])
        mx = sb("mx", [P, NT])
        top = sb("top", [P, 3, B, TB, E])
        mx2 = sb("mx2", [P, NT])
        oh = sb("oh", [P, NT + 1, E], BF16)
        sm = sb("sm", [P, NT])
        al = sb("al", [P, 2, NT])
        pay = sb("pay", [P, NT, ROW])
        fill = sb("fill", [P, ROW])
        cnt = sb("cnt", [P, 2, E], I32)
        onesf = sb("onesf", [P, E])
        end = sb("end", [P, 2, E])
        posn = sb("posn", [P, 2, NT, E])
        slot = sb("slot", [P, NT], I32)
        ge = sb("ge", [P, 5, NS + 1, E])
        es = sb("es", [P, 2, NS + 1])
        etab = sb("etab", [P, NS + 1], I32)
        gsel = sb("gsel", [P, NS + 1])
        bsel = sb("bsel", [P, NS + 1])
        zl = sb("zl", [P, LANES, ROW])
        zts = sb("zts", [P, 2, P])
        hs = sb("hs", [P, 2, F])
        hts = sb("hts", [P, 2, F])
        t2 = sb("t2", [P, LANES, D])
        fb = sb("fb", [P, 2, D])
        alane = sb("alane", [P, LANES])
        idx = sb("idx", [P, NS], I32)
        fin = sb("fin", [P, LANES, D])

        ps = ctx.enter_context(nc.psum_tensor("ps", [P, 8, 512], F32))

        s_x = [sem(f"s_x{b}") for b in range(B)]
        s_pa, s_pb, s_cf, s_cb, s_xt, s_b12, s_w1, s_w2 = [
            sem(n) for n in ("s_pa", "s_pb", "s_cf", "s_cb", "s_xt", "s_b12", "s_w1", "s_w2")]
        s_fill, s_prefill = sem("s_fill"), sem("s_prefill")
        s_const, s_bcast, s_ctx4 = sem("s_const"), sem("s_bcast"), sem("s_ctx4")
        s_kt, s_kblk, s_v4p, s_v4, s_vones = sem("s_kt"), sem("s_kblk"), sem("s_v4p"), sem("s_v4"), sem("s_vones")
        s_cent, s_cents, s_woc, s_wocs = sem("s_cent"), sem("s_cents"), sem("s_woc"), sem("s_wocs")
        s_m, s_ms = sem("s_m"), sem("s_ms")
        s_ve, s_rs, s_xn, s_xnt, s_xnts = sem("s_ve"), sem("s_rs"), sem("s_xn"), sem("s_xnt"), sem("s_xnts")
        s_xb = sem("s_xb")
        s_stok, s_max, s_split, s_nmt, s_nmts = (
            sem("s_stok"), sem("s_max"), sem("s_split"), sem("s_nmt"), sem("s_nmts"))
        s_st, s_exp, s_pv, s_o, s_ot, s_ots, s_y = (
            sem("s_st"), sem("s_exp"), sem("s_pv"), sem("s_o"), sem("s_ot"), sem("s_ots"), sem("s_y"))
        s_mv2, s_mx, s_oh, s_sm, s_ex, s_al, s_nmr, s_paya, s_z = (
            sem("s_mv2"), sem("s_mx"), sem("s_oh"), sem("s_sm"), sem("s_ex"), sem("s_al"), sem("s_nmr"),
            sem("s_paya"), sem("s_z"))
        s_rank, s_slot, s_etab, s_gsel, s_sent = (
            sem("s_rank"), sem("s_slot"), sem("s_etab"), sem("s_gsel"), sem("s_sent"))
        s_dve, s_pool = sem("s_dve"), sem("s_pool")
        s_zl = [sem(f"s_zl{j}") for j in range(LANES)]
        s_zt, s_zts, s_h, s_hs, s_ht, s_hts, s_f, s_fin, s_t2 = (
            sem("s_zt"), sem("s_zts"), sem("s_h"), sem("s_hs"), sem("s_ht"), sem("s_hts"), sem("s_f"),
            sem("s_fin"), sem("s_t2"))
        s_fb, s_sentout = sem("s_fb"), sem("s_sentout")
        s_yread = sem("s_yread")
        s_out = [sem(f"s_out{j}") for j in range(LANES)]
        CREDIT = 2

        block = ctx.enter_context(nc.Block())

        def load_tile(eng, n, lane):
            eng.wait_ge(s_t2, n + 1)
            eng.dma_start(zl[:, lane, :], rows[bass.ds(n * P, P), :]).then_inc(s_zl[lane], 16)

        @block.sync
        def _(sp):
            for b in range(B):
                sp.dma_start(xs[:, b * TB:(b + 1) * TB, :], x_tiles[b]).then_inc(s_x[b], 16)
            sp.dma_start(cfs[:, :], cf).then_inc(s_cf, 16)
            sp.dma_start(cbw[:, :], cb).then_inc(s_cb, 16)
            sp.dma_start(xts[:, :], xt).then_inc(s_xt, 16)
            sp.wait_ge(s_fill, 2)
            sp.dma_start(rows.rearrange("(s p) d -> p s d", p=P),
                         fill[:, :].unsqueeze(1).to_broadcast([P, NS, ROW])).then_inc(s_prefill, 16)
            sp.dma_start(w1s[:, :, :], w1).then_inc(s_w1, 16)
            sp.wait_ge(s_sent, 16 * NT)
            with sp.Fori(0, 3) as i:
                for j in range(4):
                    load_tile(sp, i * 4 + j, j)
            for n in range(12, NS):
                load_tile(sp, n, n % LANES)

        @block.gpsimd
        def _(pool):
            chain = [0]

            def link(ins):
                chain[0] += 1
                ins.then_inc(s_pool, 1)
                pool.wait_ge(s_pool, chain[0])

            nc.gpsimd.memset(mhalf[:, :, :], -0.5).then_inc(s_const, 1)
            nc.gpsimd.memset(fill[:, 0:ROW - 1], 0.0).then_inc(s_fill, 1)
            nc.gpsimd.memset(fill[:, ROW - 1:ROW], NOBODY).then_inc(s_fill, 1)
            nc.gpsimd.memset(oh[:, NT, :], 0.0).then_inc(s_const, 1)
            nc.gpsimd.memset(onesf[:, :], 1.0).then_inc(s_const, 1)
            pool.wait_ge(s_pa, 16)
            for b in range(B):
                c0 = PA["ctx"] + b * KV
                last = nc.gpsimd.tensor_copy(ctx4[:, b, :, :],
                                             pas[:, c0:c0 + KV].unsqueeze(1).to_broadcast([P, HC, KV]))
            last.then_inc(s_ctx4, 1)
            pool.wait_ge(s_const, 1)
            for b in range(B):
                t = slice(b * TB, (b + 1) * TB)
                pool.wait_ge(s_ve, b + 1)
                nc.gpsimd.tensor_tensor(rs[:, t], ve[:, t], mhalf[:, 0, t], ALU.pow).then_inc(s_rs, 1)
            pool.wait_ge(s_cf, 16)
            nc.gpsimd.tensor_copy(v4[:, :, :, HC * HD:].rearrange("p b c h -> p (b c) h"),
                                  cfs[:, CF["ones"]:CF["ones"] + HC].unsqueeze(1).to_broadcast([P, B * C, HC])
                                  ).then_inc(s_vones, 1)
            pool.wait_ge(s_b12, 16)
            nc.gpsimd.partition_broadcast(b12b[:, :], b12s[0:1, :], channels=P).then_inc(s_bcast, 1)
            nc.gpsimd.tensor_copy(pay[:, :, D + 3:D + 4].rearrange("p t o -> p (t o)"),
                                  cfs[:, CF["token"]:CF["token"] + NT]).then_inc(s_paya, 1)
            for b in range(B):
                t = slice(b * TB, (b + 1) * TB)
                mean = mv2[:, t, 0]
                var = mv2[:, t, 1]
                pool.wait_ge(s_mv2, b + 1)
                nc.gpsimd.tensor_scalar(u2[:, b, 0, :], var, 1.0, EPS, ALU.mult, ALU.add)
                link(nc.gpsimd.tensor_scalar(u2[:, b, 1, :], var, 1.0 + EPS, EPS * EPS, ALU.mult, ALU.add))
                link(nc.gpsimd.tensor_tensor(r2[:, b, :, :], u2[:, b, :, :], mhalf[:, :, 0:TB], ALU.pow))
                link(nc.gpsimd.tensor_scalar(nmr[:, b, 0, :], r2[:, b, 1, :], -1.0, 1.0, ALU.mult, ALU.mult))
                nc.gpsimd.tensor_tensor(nmr[:, b, 0, :], nmr[:, b, 0, :], mean, ALU.mult).then_inc(s_nmr, 1)
                pool.wait_ge(s_mx, b + 1)
                nc.gpsimd.tensor_tensor(sm[:, t], r2[:, b, 0, :], mx[:, t], ALU.mult).then_inc(s_sm, 1)
                link(nc.gpsimd.tensor_scalar(nmr[:, b, 1, :], r2[:, b, 0, :], 1.0, 1.0, ALU.mult, ALU.add))
                link(nc.gpsimd.tensor_tensor(nmr[:, b, 2, :], nmr[:, b, 1, :], r2[:, b, 1, :], ALU.mult))
                nc.gpsimd.tensor_tensor(pay[:, t, D], nmr[:, b, 2, :], u2[:, b, 1, :], ALU.mult).then_inc(s_paya, 1)
                nc.gpsimd.tensor_copy(pay[:, t, D + 1], mean).then_inc(s_paya, 1)
            pool.wait_ge(s_prefill, 16)
            pool.wait_ge(s_slot, 1)
            pool.wait_ge(s_paya, 1 + 2 * B)
            pool.wait_ge(s_al, B)
            pool.wait_ge(s_z, NT)
            for t in range(NT):
                nc.gpsimd.indirect_dma_start(
                    out=rows, out_offset=bass.IndirectOffsetOnAxis(ap=slot[:, t:t + 1], axis=0),
                    in_=pay[:, t, :], in_offset=None).then_inc(s_sent, 16)

            def add_up(n, lane):
                zrow = zl[:, lane, :]
                pool.wait_ge(s_zl[lane], (n // LANES + 1) * 16)
                pool.wait_ge(s_fin, n + 1)
                pool.wait_ge(s_zt, n + 1)
                nc.gpsimd.tensor_copy(idx[:, n:n + 1], zrow[:, D + 3:D + 4]).then_inc(s_pool, 1)
                nc.gpsimd.tensor_copy(alane[:, lane:lane + 1], zrow[:, D + 2:D + 3]).then_inc(s_pool, 1)
                nc.gpsimd.tensor_scalar(t2[:, lane, :], zrow[:, 0:D], zrow[:, D:D + 1], zrow[:, D + 1:D + 2],
                                        ALU.mult, ALU.add).then_inc(s_pool, 1)
                chain[0] += 3
                pool.wait_ge(s_pool, chain[0])
                nc.gpsimd.engine_nop().then_inc(s_t2, 1)

            def send(n, lane):
                if n >= LANES - 1:
                    m = n - (LANES - 1)
                    pool.wait_ge(s_out[m % LANES], 16 * (m // LANES + 1))
                    nc.gpsimd.engine_nop().then_inc(s_sentout, 1)
                pool.wait_ge(s_fin, n + 1 + LANES)
                nc.gpsimd.indirect_dma_start(
                    out=out_rows, out_offset=bass.IndirectOffsetOnAxis(ap=idx[:, n:n + 1], axis=0),
                    in_=fin[:, lane, :], in_offset=None, bounds_check=B * T - 1, oob_is_err=False
                ).then_inc(s_out[lane], 16)
            for n in range(NS + 3):
                if n < NS:
                    add_up(n, n % LANES)
                if n >= 3:
                    send(n - 3, (n - 3) % LANES)
            for j in range(LANES):
                pool.wait_ge(s_out[j], 16 * ((NS - 1 - j) // LANES + 1))

        @block.scalar
        def _(act):
            act.dma_start(pas[:, :], pa).then_inc(s_pa, 16)
            act.dma_start(pbs[:, :], pb).then_inc(s_pb, 16)
            act.dma_start(b12s[:, :], b12).then_inc(s_b12, 16)
            act.dma_start(w2s[:, :, :], w2).then_inc(s_w2, 16)
            act.wait_ge(s_cent, 1)
            nc.scalar.copy(cfs[:, CF["gap"]:CF["gap"] + E], ps[:, 6, 0:E]).then_inc(s_cents, 1)
            for b in range(B):
                act.wait_ge(s_m, b + 1)
                nc.scalar.copy(ms[:, b, :], ps[:, b, :]).then_inc(s_ms, 1)
                act.wait_ge(s_xnt, b + 1)
                nc.scalar.copy(xnt[:, b * T:(b + 1) * T], ps[:, 2 + b, :]).then_inc(s_xnts, 1)
            act.wait_ge(s_woc, 1)
            nc.scalar.copy(pbs[:, PB["cen"]:PB["cen"] + E], ps[:, 7, 0:E]).then_inc(s_wocs, 1)
            act.wait_ge(s_xt, 16)
            act.wait_ge(s_pb, 16)
            nc.scalar.activation(xts[:, :], xts[:, :], ACT.Identity, bias=pbs[:, PB["bo"]:PB["bo"] + 1]
                                 ).then_inc(s_xb, 1)
            for b in range(B):
                for c in range(C):
                    act.wait_ge(s_st, b * C + c + 1)
                    nc.scalar.activation(pt[:, b, c, :], ps[:, 2 + c % 2, :], ACT.Exp, scale=SCALE).then_inc(s_exp, 1)
            for b in range(B):
                act.wait_ge(s_ot, b + 1)
                nc.scalar.copy(ot[:, b, :], ps[:, b, :]).then_inc(s_ots, 1)
                yb = 6 if b == 0 else 2
                act.wait_ge(s_nmr, b + 1)
                act.wait_ge(s_yread, b + 1)
                for k in range(TB):
                    t = b * TB + k
                    y = ps[:, yb + k // 2, (k % 2) * 256:(k % 2) * 256 + D]
                    nc.scalar.activation(pay[:, t, 0:D], y, ACT.Identity, scale=r2[:, b, 1, k:k + 1],
                                         bias=nmr[:, b, 0, k:k + 1]).then_inc(s_z, 1)
                act.wait_ge(s_sm, b + 1)
                nc.scalar.activation(al[:, 0, b * TB:(b + 1) * TB], sm[:, b * TB:(b + 1) * TB], ACT.Exp,
                                     scale=-1.0).then_inc(s_ex, 1)

            def relu(n, par):
                act.wait_ge(s_ht, n + 1)
                nc.scalar.activation(hts[:, par, :], ps[:, 2 + par, :], ACT.Relu).then_inc(s_hts, 1)
            with act.Fori(0, 3) as i:
                for j in range(4):
                    relu(i * 4 + j, j % 2)
            for n in range(12, NS):
                relu(n, n % 2)

        @block.vector
        def _(dve):
            chain = [0]

            def link(ins):
                chain[0] += 1
                ins.then_inc(s_dve, 1)
                dve.wait_ge(s_dve, chain[0])

            def stats(b):
                dve.wait_ge(s_x[b], 16)
                for t in range(b * TB, (b + 1) * TB):
                    last = nc.vector.bn_stats(st[:, t, :], xs[:, t, :])
                link(last)
                for t in range(b * TB, (b + 1) * TB):
                    last = nc.vector.bn_aggr(mv[:, t, :], st[:, t, :])
                link(last)
                t = slice(b * TB, (b + 1) * TB)
                nc.vector.tensor_scalar(ve[:, t], mv[:, t, 1], EPS, None, ALU.add).then_inc(s_ve, 1)

            def normalise(b):
                dve.wait_ge(s_rs, b + 1)
                for t in range(b * TB, (b + 1) * TB):
                    last = nc.vector.tensor_scalar(xn[:, t, :], xs[:, t, :], mv[:, t, 0:1], rs[:, t:t + 1],
                                                   ALU.subtract, ALU.mult)
                last.then_inc(s_xn, 1)

            stats(0)
            dve.wait_ge(s_cf, 16)
            dve.wait_ge(s_kt, 1)
            for b in range(B):
                nc.vector.tensor_tensor(
                    kblk[:, b, :, :], ps[:, 4, b * KV:(b + 1) * KV].unsqueeze(1).to_broadcast([P, H, KV]),
                    cfs[:, CF["hmask"]:CF["hmask"] + H].unsqueeze(2).to_broadcast([P, H, KV]),
                    ALU.mult).then_inc(s_kblk, 1)
            stats(1)
            normalise(0)
            dve.wait_ge(s_v4p, 1)
            for b in range(B):
                nc.vector.tensor_tensor(
                    v4[:, b, :, 0:HC * HD], ps[:, 5, b * P:(b + 1) * P].rearrange("p (c n) -> p c n", c=C),
                    cfs[:, CF["vmask"]:CF["vmask"] + HC * HD].unsqueeze(1).to_broadcast([P, C, HC * HD]),
                    ALU.mult).then_inc(s_v4, 1)
            normalise(1)

            def head_max(b, k):
                n = b * TB + k
                dve.wait_ge(s_stok, n + 1)
                return nc.vector.tensor_reduce(nm[:, b, k, :], ps[:, n % 2, :].rearrange("p (h k) -> p h k", h=H),
                                               X, ALU.max, negate=True).then_inc(s_max, 1)

            def split(b):
                dve.wait_ge(s_max, (b + 1) * TB)
                link(nc.vector.tensor_copy(nm2[:, b, :, 0, :], nm[:, b, :, :]))
                nc.vector.tensor_tensor(nm2[:, b, :, 1, :], nm[:, b, :, :], nm2[:, b, :, 0, :],
                                        ALU.subtract).then_inc(s_split, 1)

            def shift_rows(b):
                dve.wait_ge(s_nmt, b + 1)
                nc.vector.tensor_copy(nmt[:, b, :], ps[0:2 * H, 4 + b, 0:T // 2].bitcast(BF16)).then_inc(s_nmts, 1)

            for k in range(TB):
                head_max(0, k)
            split(0)
            head_max(1, 0)
            head_max(1, 1)
            shift_rows(0)
            head_max(1, 2)
            head_max(1, 3)
            split(1)
            shift_rows(1)

            for b in range(B):
                dve.wait_ge(s_pv, b + 1)
                pv = ps[:, 4:6, :].rearrange("p a (u n) -> p (a u) n", n=64)
                link(nc.vector.reciprocal(rden[:, b, :, :], pv[:, :, HC * HD:VW]))
                nc.vector.tensor_tensor(
                    o[:, b, :].rearrange("p (u h d) -> p u h d", h=HC, d=HD),
                    pv[:, :, 0:HC * HD].rearrange("p u (h d) -> p u h d", h=HC),
                    rden[:, b, :, :].unsqueeze(3).to_broadcast([P, TB * C, HC, HD]), ALU.mult).then_inc(s_o, 1)

                t = slice(b * TB, (b + 1) * TB)
                yb = 6 if b == 0 else 2
                ys = ps[:, yb:yb + 2, :].rearrange("p a (t n) -> p (a t) n", t=2)
                dve.wait_ge(s_y, b + 1)
                for k in range(TB):
                    nc.vector.bn_stats(st2[:, b * TB + k, :], ys[:, k, 0:D])
                sc = ys[:, :, D:YW]
                nc.vector.tensor_reduce(mx[:, t], sc, X, ALU.max).then_inc(s_mx, 1)
                dve.wait_ge(s_mx, b + 1)
                nc.vector.tensor_tensor(top[:, 0, b, :, :], sc, mx[:, t].unsqueeze(2).to_broadcast([P, TB, E]),
                                        ALU.is_equal).then_inc(s_yread, 1)
                dve.wait_ge(s_yread, b + 1)
                for k in range(TB):
                    last = nc.vector.bn_aggr(mv2[:, b * TB + k, :], st2[:, b * TB + k, :])
                last.then_inc(s_mv2, 1)
                descb = desc.unsqueeze(1).to_broadcast([P, TB, E])
                link(nc.vector.tensor_tensor(top[:, 1, b, :, :], top[:, 0, b, :, :], descb, ALU.mult))
                link(nc.vector.tensor_reduce(mx2[:, t], top[:, 1, b, :, :], X, ALU.max))
                nc.vector.tensor_tensor(oh[:, t, :], descb, mx2[:, t].unsqueeze(2).to_broadcast([P, TB, E]),
                                        ALU.is_equal).then_inc(s_oh, 1)
            dve.wait_ge(s_rank, 1)
            dve.wait_ge(s_const, 3)
            rank = ps[:, 5, 0:(NT + 1) * E].rearrange("p (t e) -> p t e", e=E)
            link(nc.vector.tensor_scalar(cnt[:, 0, :], rank[:, NT, :], float(P - 1), None, ALU.add))
            link(nc.vector.tensor_scalar(cnt[:, 1, :], cnt[:, 0, :], -P, None, ALU.bitwise_and))
            link(nc.vector.tensor_tensor_scan(end[:, 0, :], onesf[:, :], cnt[:, 1, :], 0.0, ALU.mult, ALU.add))
            link(nc.vector.tensor_tensor(end[:, 1, :], end[:, 0, :], cnt[:, 1, :], ALU.subtract))
            link(nc.vector.tensor_tensor(posn[:, 0, :, :], rank[:, 0:NT, :],
                                         end[:, 1, :].unsqueeze(1).to_broadcast([P, NT, E]), ALU.add))
            link(nc.vector.tensor_tensor(posn[:, 1, :, :], posn[:, 0, :, :], oh[:, 0:NT, :], ALU.mult))
            with nc.allow_low_precision("whole numbers below 2^11"):
                nc.vector.tensor_reduce(slot[:, :], posn[:, 1, :, :], X, ALU.add).then_inc(s_slot, 1)
            for b in range(B):
                t = slice(b * TB, (b + 1) * TB)
                dve.wait_ge(s_ex, b + 1)
                link(nc.vector.tensor_scalar(al[:, 1, t], al[:, 0, t], 1.0, None, ALU.add))
                nc.vector.reciprocal(pay[:, t, D + 2], al[:, 1, t]).then_inc(s_al, 1)
            S1 = NS + 1
            link(nc.vector.tensor_tensor(ge[:, 0, :, :],
                                         cfs[:, CF["slot"]:CF["slot"] + S1].unsqueeze(2).to_broadcast([P, S1, E]),
                                         end[:, 0, :].unsqueeze(1).to_broadcast([P, S1, E]), ALU.is_ge))
            link(nc.vector.tensor_reduce(es[:, 0, :], ge[:, 0, :, :], X, ALU.add))
            link(nc.vector.tensor_scalar(es[:, 1, :], es[:, 0, :], float(E - 1), None, ALU.min))
            nc.vector.tensor_copy(etab[:, :], es[:, 1, :]).then_inc(s_etab, 1)
            link(nc.vector.tensor_tensor(ge[:, 1, :, :], es[:, 1, :].unsqueeze(2).to_broadcast([P, S1, E]),
                                         cfs[:, CF["expert"]:CF["expert"] + E].unsqueeze(1).to_broadcast([P, S1, E]),
                                         ALU.is_equal))
            for k, name in ((2, "gam"), (3, "bet")):
                link(nc.vector.tensor_tensor(ge[:, k, :, :], ge[:, 1, :, :],
                                             pbs[:, PB[name]:PB[name] + E].unsqueeze(1).to_broadcast([P, S1, E]),
                                             ALU.mult))
                link(nc.vector.tensor_reduce((gsel if k == 2 else bsel)[:, :], ge[:, k, :, :], X, ALU.add))
            dve.wait_ge(s_bcast, 1)
            nc.vector.engine_nop().then_inc(s_t2, LANES)
            nc.vector.engine_nop().then_inc(s_fin, LANES)
            nc.vector.engine_nop().then_inc(s_sentout, LANES)
            nc.vector.engine_nop().then_inc(s_zts, CREDIT)
            nc.vector.engine_nop().then_inc(s_hs, CREDIT)

            def scale_shift(n, par):
                dve.wait_ge(s_zt, n + 1)
                nc.vector.tensor_scalar(zts[:, par, :], ps[:, 6 + par, 0:P], gsel[:, bass.ds(n, 1)],
                                        bsel[:, bass.ds(n, 1)], ALU.mult, ALU.add).then_inc(s_zts, 1)

            def add_bias(n, par, e):
                dve.wait_ge(s_h, n + 1)
                nc.vector.tensor_tensor(hs[:, par, :], ps[:, par, :],
                                        b1b[:, bass.ds(e, 1), :].rearrange("p a n -> p (a n)"),
                                        ALU.add).then_inc(s_hs, 1)

            def finish(n, par, lane, e):
                dve.wait_ge(s_f, n + 1)
                dve.wait_ge(s_t2, n + 1 + LANES)
                dve.wait_ge(s_sentout, n + 1)
                nc.vector.tensor_tensor(fb[:, par, :], ps[:, 4 + par, 0:D],
                                        b2b[:, bass.ds(e, 1), :].rearrange("p a n -> p (a n)"),
                                        ALU.add).then_inc(s_fb, 1)
                dve.wait_ge(s_fb, n + 1)
                nc.vector.scalar_tensor_tensor(fin[:, lane, :], fb[:, par, :], alane[:, lane:lane + 1],
                                               t2[:, lane, :], ALU.mult, ALU.add).then_inc(s_fin, 1)

            scale_shift(0, 0)
            for s in range(2):
                scale_shift(s + 1, (s + 1) % 2)
                e = dve.value_load(etab[0:1, s:s + 1], min_val=0, max_val=E - 1)
                add_bias(s, s % 2, e)
            regs = [dve.alloc_register(name=f"dve_expert{k}") for k in range(6)]
            with dve.Fori(0, 3) as i:
                dve.load(regs, etab[0:1, bass.ds(i * 4, 6)])
                ee = [dve.snap(r, min_val=0, max_val=E - 1) for r in regs]
                for j in range(4):
                    s = i * 4 + 2 + j
                    scale_shift(s + 1, (j + 1) % 2)
                    add_bias(s, j % 2, ee[j + 2])
                    finish(i * 4 + j, j % 2, j, ee[j])
            ee = [dve.value_load(etab[0:1, n:n + 1], min_val=0, max_val=E - 1) for n in range(12, NS)]
            add_bias(NS - 1, (NS - 1) % 2, ee[2])
            for n in range(12, NS):
                finish(n, n % 2, n % LANES, ee[n - 12])

        @block.tensor
        def _(pe):
            mm = nc.tensor.matmul
            pe.wait_ge(s_pa, 16)
            mm(ps[:, 4, 0:B * KV], pas[:, 0:P], pas[:, PA["ctx"]:PA["ctx"] + B * KV],
               start=True, stop=True).then_inc(s_kt, 1)
            pe.wait_ge(s_ctx4, 1)
            for b in range(B):
                last = mm(ps[:, 5, b * P:(b + 1) * P],
                          ctx4[:, b, :, :].rearrange("p r k -> p (r k)"),
                          pas[:, PA["wv"]:PA["wv"] + P], start=True, stop=True)
            last.then_inc(s_v4p, 1)
            pe.wait_ge(s_cf, 16)
            pe.wait_ge(s_pb, 16)
            mm(ps[:, 6, 0:E], cfs[:, CF["center"]:CF["center"] + P], pbs[:, PB["cen"]:PB["cen"] + E],
               start=True, stop=True).then_inc(s_cent, 1)
            for b in range(B):
                pe.wait_ge(s_kblk, b + 1)
                mm(ps[:, b, :], pas[:, PA["wq"]:PA["wq"] + P], kblk[:, b, :, :].rearrange("p h k -> p (h k)"),
                   start=True, stop=True).then_inc(s_m, 1)
                pe.wait_ge(s_xn, b + 1)
                for k in range(TB):
                    last = nc.tensor.transpose(ps[:, 2 + b, k * P:(k + 1) * P], xn[:, b * TB + k, :], ident)
                last.then_inc(s_xnt, 1)
            pe.wait_ge(s_cents, 1)
            mm(ps[:, 7, 0:E], pbs[:, PB["wo"]:PB["wo"] + P], cfs[:, CF["gap"]:CF["gap"] + E],
               start=True, stop=True).then_inc(s_woc, 1)

            pe.wait_ge(s_cb, 16)
            causal = cbs[0:KV, CB["causal"]:CB["causal"] + P]

            def scores(b, k):
                n = b * TB + k
                pe.wait_ge(s_ms, b + 1)
                pe.wait_ge(s_xnts, b + 1)
                if n < 2:
                    pe.wait_ge(s_ms, n + 1)
                else:
                    pe.wait_ge(s_max, n - 1)
                last = mm(ps[:, n % 2, :], xnt[:, n * P:(n + 1) * P], ms[:, b, :], start=True, stop=k > 0)
                if k == 0:
                    last = mm(ps[:, n % 2, :].rearrange("p (c n) -> p c n", c=C), identb[0:KV, :],
                              causal.unsqueeze(1).to_broadcast([KV, C, P]), start=False, stop=True)
                last.then_inc(s_stok, 1)

            def shift_cols(b):
                pe.wait_ge(s_split, b + 1)
                for k in range(TB):
                    last = nc.tensor.transpose(ps[0:2 * H, 4 + b, k * 64:(k + 1) * 64].bitcast(BF16),
                                               nm2[:, b, k, :, :].rearrange("p a h -> p (a h)"), identb)
                last.then_inc(s_nmt, 1)

            def scores_t(b, c):
                n = b * C + c
                if n >= 2:
                    pe.wait_ge(s_exp, n - 1)
                pe.wait_ge(s_nmts, b + 1)
                bank = ps[:, 2 + c % 2, :]
                mm(bank, ms[:, b, c * P:(c + 1) * P], xnt[:, b * T:(b + 1) * T], start=True, stop=False)
                mm(bank[:, 0:KV], causal, identb[0:KV, 0:KV], start=False, stop=False)
                mm(bank, cbs[0:2 * H, CB["spread"] + c * P:CB["spread"] + (c + 1) * P], nmt[:, b, :],
                   start=False, stop=True).then_inc(s_st, 1)

            def weigh(b, c):
                pe.wait_ge(s_exp, b * C + c + 1)
                for k in range(TB):
                    u = k * C + c
                    last = mm(ps[:, 4 + u // 8, (u % 8) * 64:(u % 8) * 64 + VW], pt[:, b, c, k * P:(k + 1) * P],
                              v4[:, b, c, :], start=True, stop=True)
                if c == C - 1:
                    last.then_inc(s_pv, 1)

            def project(b):
                pe.wait_ge(s_o, b + 1)
                for k in range(TB):
                    last = nc.tensor.transpose(ps[:, b, k * P:(k + 1) * P], o[:, b, k * P:(k + 1) * P], ident)
                last.then_inc(s_ot, 1)
                yb = 6 if b == 0 else 2
                pe.wait_ge(s_xb, 1)
                pe.wait_ge(s_wocs, 1)
                pe.wait_ge(s_ots, b + 1)
                for k in range(TB):
                    y = ps[:, yb + k // 2, (k % 2) * 256:(k % 2) * 256 + YW]
                    mm(y, xts[:, (b * TB + k) * P:(b * TB + k + 1) * P], identc, start=True, stop=False)
                    last = mm(y, ot[:, b, k * P:(k + 1) * P], wo_ext, start=False, stop=True)
                last.then_inc(s_y, 1)

            for k in range(TB):
                scores(0, k)
            scores(1, 0)
            scores(1, 1)
            shift_cols(0)
            scores(1, 2)
            scores(1, 3)
            for c in range(C):
                scores_t(0, c)
            shift_cols(1)
            pe.wait_ge(s_v4, B)
            pe.wait_ge(s_vones, 1)
            pe.wait_ge(s_nmts, B)
            for c in range(C):
                scores_t(1, c)
                weigh(0, c)
            project(0)
            pe.wait_ge(s_o, 1)
            for c in range(C):
                weigh(1, c)
            project(1)
            pe.wait_ge(s_oh, B)
            pe.wait_ge(s_const, 3)
            pe.wait_ge(s_o, B)
            rank = ps[:, 5, 0:(NT + 1) * E].rearrange("p (t e) -> p t e", e=E)
            mm(rank, cbs[:, CB["before"]:CB["before"] + P], oh[:, :, :], start=True, stop=False)
            for t in range(NT):
                last = mm(rank[:, t + 1:, :], cbs[:, CB["ones"]:CB["ones"] + P],
                          oh[:, t:t + 1, :].to_broadcast([P, NT - t, E]), start=False, stop=t == NT - 1)
            last.then_inc(s_rank, 1)

            def turn(n, par, lane, seen):
                pe.wait_ge(s_zl[lane], seen * 16 + 16)
                pe.wait_ge(s_zts, n + 1)
                nc.tensor.transpose(ps[:, 6 + par, 0:P], zl[:, lane, 0:D], ident).then_inc(s_zt, 1)

            def first(n, par, e):
                pe.wait_ge(s_zts, n + 1 + CREDIT)
                pe.wait_ge(s_hs, n + 1)
                mm(ps[:, par, :], zts[:, par, :], w1s[:, bass.ds(e, 1), :].rearrange("p a n -> p (a n)"),
                   start=True, stop=True).then_inc(s_h, 1)

            def turn_h(n, par):
                pe.wait_ge(s_hs, n + 1 + CREDIT)
                for c in range(FC):
                    last = nc.tensor.transpose(ps[:, 2 + par, c * P:(c + 1) * P], hs[:, par, c * P:(c + 1) * P], ident)
                last.then_inc(s_ht, 1)

            def second(n, par, e):
                pe.wait_ge(s_hts, n + 1)
                pe.wait_ge(s_fin, n + 1 + LANES - 2)
                for c in range(FC):
                    last = mm(ps[:, 4 + par, 0:D], hts[:, par, c * P:(c + 1) * P],
                              w2s[:, bass.ds(e, 1), c * D:(c + 1) * D].rearrange("p a n -> p (a n)"),
                              start=c == 0, stop=c == FC - 1)
                last.then_inc(s_f, 1)

            pe.wait_ge(s_etab, 1)
            pe.wait_ge(s_w1, 16)
            pe.wait_ge(s_w2, 16)
            turn(0, 0, 0, 0)
            turn(1, 1, 1, 0)
            e = pe.value_load(etab[0:1, 0:1], min_val=0, max_val=E - 1)
            first(0, 0, e)
            turn(2, 0, 2, 0)
            e = pe.value_load(etab[0:1, 1:2], min_val=0, max_val=E - 1)
            first(1, 1, e)
            turn_h(0, 0)
            regs = [pe.alloc_register(name=f"pe_expert{k}") for k in range(6)]
            with pe.Fori(0, 3) as i:
                pe.load(regs, etab[0:1, bass.ds(i * 4, 6)])
                ee = [pe.snap(r, min_val=0, max_val=E - 1) for r in regs]
                for j in range(4):
                    s = i * 4 + 2 + j
                    turn(s + 1, (j + 1) % 2, (3 + j) % LANES, i + (3 + j) // LANES)
                    first(s, j % 2, ee[j + 2])
                    turn_h(s - 1, (j + 1) % 2)
                    second(s - 2, j % 2, ee[j])
            ee = [pe.value_load(etab[0:1, n:n + 1], min_val=0, max_val=E - 1) for n in range(12, NS)]
            first(14, 0, ee[2])
            turn_h(13, 1)
            second(12, 0, ee[0])
            turn_h(14, 0)
            second(13, 1, ee[1])
            second(14, 0, ee[2])


def constants():
    import numpy as np
    cf = np.zeros((P, CF_W), np.float32)
    r = np.arange(P)
    cf[:, CF["ident"]:CF["ident"] + P] = np.eye(P)
    cf[:, CF["center"]:CF["center"] + P] = np.eye(P) - 1.0 / D
    cf[:, CF["hmask"]:CF["hmask"] + H] = r[:, None] // HD == np.arange(H)[None]
    cf[:, CF["vmask"]:CF["vmask"] + HC * HD] = r[:, None] // KV == np.arange(HC * HD)[None] // HD
    cf[:, CF["ones"]:CF["ones"] + HC] = r[:, None] // KV == np.arange(HC)[None]
    cf[:, CF["desc"]:CF["desc"] + E] = E - np.arange(E)[None]
    cf[:, CF["token"]:CF["token"] + NT] = r[:, None] + P * np.arange(NT)[None]
    cf[:, CF["expert"]:CF["expert"] + E] = np.arange(E)[None]
    cf[:, CF["slot"]:CF["slot"] + NS + 1] = P * np.arange(NS + 1)[None]
    cb = np.zeros((P, CB_W), np.float32)
    cb[:, CB["ident"]:CB["ident"] + P] = np.eye(P)
    cb[:, CB["before"]:CB["before"] + P] = r[:, None] < r[None]
    cb[:, CB["ones"]:CB["ones"] + P] = 1.0
    rows = np.arange(2 * H)[:, None] % H
    cb[0:2 * H, CB["spread"]:CB["spread"] + C * P] = rows == np.arange(C * P)[None] // KV
    cb[0:KV, CB["causal"]:CB["causal"] + P] = np.where(np.arange(P)[None] % KV > np.arange(KV)[:, None], NEG, 0.0)
    return cf, (cb.view(np.uint32) >> 16).astype(np.uint16)


def kernel(x, ctx_1024, L0_xattn_Wq, L0_xattn_Wk, L0_xattn_Wv, L0_xattn_Wo, L0_xattn_bo, L0_ffn_centroids,
           L0_ffn_gamma, L0_ffn_beta, L0_ffn_W1, L0_ffn_b1, L0_ffn_W2, L0_ffn_b2):
    import numpy as np
    import concourse.bacc as bacc
    from concourse import mybir as mb
    from concourse.bass_utils import run_bass_kernel_spmd as run

    def a(v):
        return np.asarray(v)
    cf, cb = constants()
    arrays = {
        "x": np.ascontiguousarray(a(x)),
        "xt": np.ascontiguousarray(a(x).reshape(B * T, D).T),
        "pa": np.ascontiguousarray(np.concatenate([
            a(L0_xattn_Wk).T, a(ctx_1024).reshape(B * KV, D).T, a(L0_xattn_Wv).T, a(L0_xattn_Wq)], axis=1)),
        "pb": np.ascontiguousarray(np.concatenate([
            a(L0_xattn_Wo), a(L0_xattn_Wo).T, a(L0_ffn_centroids).T, a(L0_ffn_gamma).T, a(L0_ffn_beta).T,
            a(L0_xattn_bo)[:, None]], axis=1)),
        "cf": cf,
        "cb": cb,
        "b12": np.ascontiguousarray(np.concatenate([a(L0_ffn_b1).reshape(1, -1), a(L0_ffn_b2).reshape(1, -1)], axis=1)),
        "w1": np.ascontiguousarray(a(L0_ffn_W1).transpose(2, 0, 1)),
        "w2": np.ascontiguousarray(a(L0_ffn_W2).reshape(E, D, FC, P).transpose(3, 0, 2, 1).reshape(P, E, FC * D)),
    }
    nc = bacc.Bacc("TRN2", target_bir_lowering=False, num_devices=1)
    aps = [nc.dram_tensor(f"in_{k}", v.shape, mb.dt.from_np(v.dtype), kind="ExternalInput").ap()
           for k, v in arrays.items()]
    out = nc.dram_tensor("out", (B, T, D), mb.dt.float32, kind="ExternalOutput").ap()
    xattn_moe(nc, *aps, out)
    r = run(nc, [{f"in_{k}": v for k, v in arrays.items()}], core_ids=[0])
    return r.results[0]["out"]
```

```python
from contextlib import ExitStack

import concourse.bass as bass
from concourse import mybir

F32 = mybir.dt.float32
BF16 = mybir.dt.bfloat16
I32 = mybir.dt.int32
ALU = mybir.AluOpType
ACT = mybir.ActivationFunctionType
X = mybir.AxisListType.X

P = 128
B, T, D = 2, 512, 128
TB = T // P
NT = B * TB
KV = 32
H, HD = 16, 8
HC = P // KV
C = H // HC
E, F = 8, 512
FC = F // P
EPS = 1e-5
SCALE = float(HD) ** -0.5
NEG = -1e37
NS = NT + E - 1
ROW = D + 3
LANES = 4
VW = HC * HD + HC
OT = (0, 1), (1, 6)
YW = D + E
STOK = (0, 1, 5)
NOBODY = 4096

PA = dict(wk=0, ctx=128, wv=192, wq=320)
PA_W = 448
PB = dict(wo=0, wot=128, cen=256, gam=264, bet=272, b1=280, bo=312)
PB_W = 313
CF = dict(ident=0, gap=128, center=136, hmask=264, vmask=280, ones=312, desc=316, code=324, expert=332, slot=340, row=356)
CF_W = 357
CB = dict(ident=0, before=128, ones=256, spread=384, causal=896, lane=1024)
CB_W = 1152


def xattn_moe(nc, x, xt, pa, pb, cf, cb, b2, w1, w2, out):
    rows = nc.dram_tensor("token_rows", [B * T, ROW], F32, kind="Internal").ap()
    row_tiles = rows.rearrange("(b t p) d -> b p t d", b=B, p=P)
    out_rows = out.rearrange("b t d -> (b t) d")
    x_tiles = x.rearrange("b (t p) d -> b p t d", p=P)
    ctx = ExitStack()
    with ctx:
        def sb(name, shape, dt=F32):
            return ctx.enter_context(nc.sbuf_tensor(name, shape, dt))

        def sem(name):
            return ctx.enter_context(nc.semaphore(name))

        xs = sb("xs", [P, NT, D])
        xts = sb("xts", [P, NT * P])
        pas = sb("pas", [P, PA_W])
        pbs = sb("pbs", [P, PB_W])
        cfs = sb("cfs", [P, CF_W])
        cbw = sb("cbw", [P, CB_W], mybir.dt.uint16)
        cbs = cbw[:, :].bitcast(BF16)
        b2s = sb("b2s", [1, E * D])
        w1s = sb("w1s", [P, E, F])
        w2s = sb("w2s", [P, E, FC * D])
        b2b = sb("b2b", [P, E, D])
        b1t = pbs[:, PB["b1"]:PB["b1"] + E * FC].rearrange("p (e c) -> p e c", e=E)
        ident = cfs[:, 0:P]
        identb = cbs[:, 0:P]
        identc = cfs[:, 0:YW]
        wo_ext = pbs[:, PB["wot"]:PB["wot"] + YW]
        desc = cfs[:, CF["desc"]:CF["desc"] + E]
        kblk = sb("kblk", [P, B, H, KV])
        ctx4 = sb("ctx4", [P, B, HC, KV])
        v4 = sb("v4", [P, B, C, VW])
        ms = sb("ms", [P, B, H * KV])
        st = sb("st", [P, NT, 6])
        mv = sb("mv", [P, NT, 2])
        ve = sb("ve", [P, NT])
        sd = sb("sd", [P, NT])
        rs = sb("rs", [P, NT])
        filler = sb("filler", [P, 512], BF16)
        tiny = sb("tiny", [P, 4])
        xn = sb("xn", [P, NT, D])
        xnt = sb("xnt", [P, NT * P])
        nm = sb("nm", [P, B, TB, H])
        nm2 = sb("nm2", [P, B, TB, 2, H], BF16)
        nmt = sb("nmt", [2 * H, B, T], BF16)
        pt = sb("pt", [P, B, C, T])
        rden = sb("rden", [P, B, TB * C, HC])
        o = sb("o", [P, B, T])
        ot = sb("ot", [P, B, T])
        st2 = sb("st2", [P, NT, 6])
        mv2 = sb("mv2", [P, NT, 2])
        u2 = sb("u2", [P, B, 2, TB])
        sd2 = sb("sd2", [P, B, 2, TB])
        r2 = sb("r2", [P, B, 2, TB])
        nmr = sb("nmr", [P, B, TB])
        mx = sb("mx", [P, NT])
        top = sb("top", [P, 3, B, TB, E])
        mx2 = sb("mx2", [P, NT])
        oh = sb("oh", [P, NT + 1, E], BF16)
        pay = sb("pay", [P, NT, ROW])
        cnt = sb("cnt", [P, 2, E], I32)
        onesf = sb("onesf", [P, E])
        end = sb("end", [P, 2, E])
        mine = sb("mine", [P, NT, E])
        rank = sb("rank", [P, NT], I32)
        low = sb("low", [P, NT], I32)
        high = sb("high", [P, NT], I32)
        row_oh = sb("row_oh", [P, NT, P], BF16)
        base = sb("base", [P, NT, E])
        first_slot = sb("first_slot", [P, NT])
        tile = sb("tile", [P, NT])
        tile_oh = sb("tile_oh", [P, NT, NS])
        tile_code = sb("tile_code", [P, 2, NT, NS], BF16)
        idx = sb("idx", [P, NS], I32)
        ge = sb("ge", [P, 5, NS + 1, E])
        es = sb("es", [P, 2, NS + 1])
        etab = sb("etab", [P, NS + 1], I32)
        gsel = sb("gsel", [P, NS + 1])
        bsel = sb("bsel", [P, NS + 1])
        zl = sb("zl", [P, LANES, ROW])
        zts = sb("zts", [P, 2, P])
        w1c = sb("w1c", [P, 2, F])
        hs = sb("hs", [P, 2, F])
        hts = sb("hts", [P, 2, F])
        t2 = sb("t2", [P, NS, D])
        alpha = sb("alpha", [P, NS])
        fb = sb("fb", [P, 2, D])
        fin = sb("fin", [P, NS, D])

        ps = ctx.enter_context(nc.psum_tensor("ps", [P, 8, 512], F32))

        def sems(names):
            return [sem(n) for n in names.split()]

        s_x = [sem(f"s_x{b}") for b in range(B)]
        s_pa, s_pb, s_cf, s_cb, s_xt, s_b2, s_w1, s_w2 = sems("s_pa s_pb s_cf s_cb s_xt s_b2 s_w1 s_w2")
        s_filler = sem("s_filler")
        s_blank, s_const, s_bcast, s_ctx4, s_kt, s_kblk, s_v4p, s_v4, s_vones = sems(
            "s_blank s_const s_bcast s_ctx4 s_kt s_kblk s_v4p s_v4 s_vones")
        s_cent, s_cents, s_woc, s_wocs, s_m, s_ms, s_xb = sems("s_cent s_cents s_woc s_wocs s_m s_ms s_xb")
        s_ve, s_sd, s_xn, s_xnt, s_xnts = sems("s_ve s_sd s_xn s_xnt s_xnts")
        s_stok, s_max, s_split, s_nmt, s_nmts = sems("s_stok s_max s_split s_nmt s_nmts")
        s_st, s_exp, s_pv, s_o, s_ot, s_ots, s_y = sems("s_st s_exp s_pv s_o s_ot s_ots s_y")
        s_oh, s_u2, s_sd2, s_nmr, s_paya, s_za, s_zd, s_rank, s_row_oh, s_tile_oh, s_ids, s_idx, s_etab, s_written = sems(
            "s_oh s_u2 s_sd2 s_nmr s_paya s_za s_zd s_rank s_row_oh s_tile_oh s_ids s_idx s_etab s_written")
        s_zl = [sem(f"s_zl{j}") for j in range(LANES)]
        s_zt, s_zts, s_w1c, s_h, s_hs, s_hts, s_f, s_fb, s_fin, s_t2, s_out = sems(
            "s_zt s_zts s_w1c s_h s_hs s_hts s_f s_fb s_fin s_t2 s_out")
        s_dve = sem("s_dve")
        CREDIT = 2

        block = ctx.enter_context(nc.Block())

        @block.sync
        def _(sp):
            sp.dma_start(xs[:, 0:TB, :], x_tiles[0]).then_inc(s_x[0], 16)
            sp.dma_start(cfs[:, :], cf).then_inc(s_cf, 16)
            sp.dma_start(xs[:, TB:, :], x_tiles[1]).then_inc(s_x[1], 16)
            sp.dma_start(pbs[:, :], pb).then_inc(s_pb, 16)
            sp.dma_start(xts[:, :], xt).then_inc(s_xt, 16)
            sp.dma_start(cbw[:, :], cb).then_inc(s_cb, 16)
            sp.dma_start(b2s[:, :], b2).then_inc(s_b2, 16)
            sp.dma_start(w1s[:, :, :], w1).then_inc(s_w1, 16)
            sp.dma_start(w2s[:, :, :], w2).then_inc(s_w2, 16)
            for b in range(B):
                sp.wait_ge(s_paya, b + 1)
                sp.wait_ge(s_za, b + 1)
                sp.wait_ge(s_zd, b + 1)
                sp.dma_start(row_tiles[b], pay[:, b * TB:(b + 1) * TB, :]).then_inc(s_written, 16)

        @block.gpsimd
        def _(pool):
            nc.gpsimd.memset(tiny[:, :], 1.0).then_inc(s_const, 1)
            nc.gpsimd.memset(oh[:, NT, :], 0.0)
            nc.gpsimd.memset(onesf[:, :], 1.0).then_inc(s_const, 1)
            pool.wait_ge(s_pa, 16)
            for b in range(B):
                c0 = PA["ctx"] + b * KV
                last = nc.gpsimd.tensor_copy(ctx4[:, b, :, :],
                                             pas[:, c0:c0 + KV].unsqueeze(1).to_broadcast([P, HC, KV]))
            last.then_inc(s_ctx4, 1)
            pool.wait_ge(s_cf, 16)
            nc.gpsimd.tensor_copy(v4[:, :, :, HC * HD:].rearrange("p b c h -> p (b c) h"),
                                  cfs[:, CF["ones"]:CF["ones"] + HC].unsqueeze(1).to_broadcast([P, B * C, HC])
                                  ).then_inc(s_vones, 1)
            nc.gpsimd.memset(zl[:, :, :], 0.0).then_inc(s_blank, 1)
            pool.wait_ge(s_b2, 16)
            nc.gpsimd.partition_broadcast(b2b[:, :, :].rearrange("p e d -> p (e d)"), b2s[0:1, :],
                                          channels=P).then_inc(s_bcast, 1)
            pool.wait_ge(s_blank, 1)
            pool.wait_ge(s_idx, 1)
            pool.wait_ge(s_written, 16 * B)

            def gather(n):
                if n >= LANES:
                    pool.wait_ge(s_zl[n % LANES], 16 * (n // LANES))
                    pool.wait_ge(s_zt, n - LANES + 1)
                    pool.wait_ge(s_t2, n - LANES + 1)
                nc.gpsimd.indirect_dma_start(
                    out=zl[:, n % LANES, :], out_offset=None,
                    in_=rows, in_offset=bass.IndirectOffsetOnAxis(ap=idx[:, n:n + 1], axis=0),
                    bounds_check=B * T - 1, oob_is_err=False).then_inc(s_zl[n % LANES], 16)

            def send(n):
                pool.wait_ge(s_fin, n + 1)
                nc.gpsimd.indirect_dma_start(
                    out=out_rows, out_offset=bass.IndirectOffsetOnAxis(ap=idx[:, n:n + 1], axis=0),
                    in_=fin[:, n, :], in_offset=None, bounds_check=B * T - 1, oob_is_err=False).then_inc(s_out, 16)

            for n in range(NS + 6):
                if n < NS:
                    gather(n)
                if n >= 6:
                    send(n - 6)
            pool.wait_ge(s_out, 16 * NS)

        @block.scalar
        def _(act):
            act.dma_start(pas[:, :], pa).then_inc(s_pa, 16)
            act.wait_ge(s_const, 1)
            nc.scalar.activation(tiny[:, 1:2], tiny[:, 0:1], ACT.Sqrt)

            def std(b):
                act.wait_ge(s_ve, b + 1)
                t = slice(b * TB, (b + 1) * TB)
                nc.scalar.activation(sd[:, t], ve[:, t], ACT.Sqrt).then_inc(s_sd, 1)

            std(0)
            act.wait_ge(s_cent, 1)
            nc.scalar.copy(cfs[:, CF["gap"]:CF["gap"] + E], ps[:, 0, 0:E]).then_inc(s_cents, 1)
            act.wait_ge(s_m, 1)
            nc.scalar.copy(ms[:, 0, :], ps[:, 6, :]).then_inc(s_ms, 1)
            act.wait_ge(s_xnt, 1)
            nc.scalar.copy(xnt[:, 0:T], ps[:, 2, :]).then_inc(s_xnts, 1)
            act.wait_ge(s_woc, 1)
            nc.scalar.copy(pbs[:, PB["cen"]:PB["cen"] + E], ps[:, 1, 0:E]).then_inc(s_wocs, 1)
            std(1)
            act.wait_ge(s_m, 2)
            nc.scalar.copy(ms[:, 1, :], ps[:, 7, :]).then_inc(s_ms, 1)
            act.wait_ge(s_xnt, 2)
            nc.scalar.copy(xnt[:, T:], ps[:, 3, :]).then_inc(s_xnts, 1)
            act.wait_ge(s_xt, 16)
            act.wait_ge(s_pb, 16)
            nc.scalar.activation(xts[:, :], xts[:, :], ACT.Identity, bias=pbs[:, PB["bo"]:PB["bo"] + 1]
                                 ).then_inc(s_xb, 1)
            nc.scalar.activation(tiny[:, 2:3], tiny[:, 0:1], ACT.Exp)
            for b in range(B):
                for c in range(C):
                    act.wait_ge(s_st, b * C + c + 1)
                    nc.scalar.activation(pt[:, b, c, :], ps[:, 2 + c % 2, :], ACT.Exp, scale=SCALE).then_inc(s_exp, 1)
            nc.scalar.activation(tiny[:, 1:2], tiny[:, 0:1], ACT.Sqrt)
            for b in range(B):
                for a in range(2):
                    act.wait_ge(s_ot, b * 2 + a + 1)
                    h = slice(a * T // 2, (a + 1) * T // 2)
                    nc.scalar.copy(ot[:, b, h], ps[:, OT[b][a], 0:T // 2]).then_inc(s_ots, 1)
                act.wait_ge(s_u2, b + 1)
                nc.scalar.activation(sd2[:, b, :, :], u2[:, b, :, :], ACT.Sqrt).then_inc(s_sd2, 1)
                yb = 6 if b == 0 else 2
                act.wait_ge(s_nmr, b + 1)
                for k in range(2):
                    last = nc.scalar.activation(pay[:, b * TB + k, 0:D],
                                                ps[:, yb + k // 2, (k % 2) * 256:(k % 2) * 256 + D], ACT.Identity,
                                                scale=r2[:, b, 1, k:k + 1], bias=nmr[:, b, k:k + 1])
                last.then_inc(s_za, 1)
            nc.scalar.activation(tiny[:, 3:4], tiny[:, 0:1], ACT.Sigmoid)
            act.wait_ge(s_etab, 1)
            act.wait_ge(s_w1, 16)

            def stage(n, par, lane, seen, e, later=True):
                if later:
                    act.wait_ge(s_h, n - 1)
                nc.scalar.copy(w1c[:, par, :], w1s[:, bass.ds(e, 1), :].rearrange("p a n -> p (a n)")
                               ).then_inc(s_w1c, 1)
                act.wait_ge(s_zl[lane], seen * 16 + 16)
                zrow = zl[:, lane, :]
                nc.scalar.activation(alpha[:, bass.ds(n, 1)], zrow[:, D + 2:D + 3], ACT.Sigmoid)
                nc.scalar.activation(t2[:, bass.ds(n, 1), :].rearrange("p a n -> p (a n)"), zrow[:, 0:D], ACT.Identity,
                                     scale=zrow[:, D:D + 1], bias=zrow[:, D + 1:D + 2]).then_inc(s_t2, 1)

            def relu(n, par):
                act.wait_ge(s_hs, n + 1 + CREDIT)
                act.wait_ge(s_f, n + 1)
                nc.scalar.activation(hts[:, par, :], hs[:, par, :], ACT.Relu).then_inc(s_hts, 1)

            regs = [act.alloc_register(name=f"act_end{k}") for k in range(3)]
            act.load(regs[0:2], etab[0:1, 0:2])
            act.load(regs[2:3], etab[0:1, NS - 1:NS])
            e_end = [act.snap(r, min_val=0, max_val=E - 1) for r in regs]
            for n in range(2):
                stage(n, n, n, 0, e_end[n], later=False)
            regs = [act.alloc_register(name=f"act_expert{k}") for k in range(4)]
            with act.Fori(0, 3) as i:
                act.load(regs, etab[0:1, bass.ds(i * 4 + 2, 4)])
                ee = [act.snap(r, min_val=0, max_val=E - 1) for r in regs]
                for j in range(4):
                    stage(i * 4 + 2 + j, j % 2, (2 + j) % LANES, i + (2 + j) // LANES, ee[j])
                    relu(i * 4 + j, j % 2)
            stage(NS - 1, 0, (NS - 1) % LANES, (NS - 1) // LANES, e_end[2])
            for n in range(12, NS):
                relu(n, n % 2)

        @block.vector
        def _(dve):
            chain = [0]

            def ranks(b):
                return ps[:, 0 if b == 0 else 5, 0:TB * E].rearrange("p (t e) -> p t e", e=E)

            def link(ins):
                chain[0] += 1
                ins.then_inc(s_dve, 1)
                dve.wait_ge(s_dve, chain[0])

            def link_both(one, two):
                one.then_inc(s_dve, 1)
                two.then_inc(s_dve, 1)
                chain[0] += 2
                dve.wait_ge(s_dve, chain[0])

            def stats(b):
                dve.wait_ge(s_x[b], 16)
                for t in range(b * TB, (b + 1) * TB):
                    last = nc.vector.bn_stats(st[:, t, :], xs[:, t, :])
                link(last)
                for t in range(b * TB, (b + 1) * TB):
                    last = nc.vector.bn_aggr(mv[:, t, :], st[:, t, :])
                link(last)
                t = slice(b * TB, (b + 1) * TB)
                nc.vector.tensor_scalar(ve[:, t], mv[:, t, 1], EPS, None, ALU.add).then_inc(s_ve, 1)

            def normalise(b):
                dve.wait_ge(s_sd, b + 1)
                link(nc.vector.reciprocal(rs[:, b * TB:(b + 1) * TB], sd[:, b * TB:(b + 1) * TB]))
                for t in range(b * TB, (b + 1) * TB):
                    last = nc.vector.tensor_scalar(xn[:, t, :], xs[:, t, :], mv[:, t, 0:1], rs[:, t:t + 1],
                                                   ALU.subtract, ALU.mult)
                last.then_inc(s_xn, 1)

            def spread_keys(b):
                nc.vector.tensor_tensor(
                    kblk[:, b, :, :], ps[:, 4, b * KV:(b + 1) * KV].unsqueeze(1).to_broadcast([P, H, KV]),
                    cfs[:, CF["hmask"]:CF["hmask"] + H].unsqueeze(2).to_broadcast([P, H, KV]),
                    ALU.mult).then_inc(s_kblk, 1)

            nc.vector.memset(filler[:, :], 0.0).then_inc(s_filler, 1)
            stats(0)
            dve.wait_ge(s_cf, 16)
            dve.wait_ge(s_kt, 1)
            spread_keys(0)
            normalise(0)
            spread_keys(1)
            stats(1)
            dve.wait_ge(s_v4p, 1)
            for b in range(B):
                nc.vector.tensor_tensor(
                    v4[:, b, :, 0:HC * HD], ps[:, 5, b * P:(b + 1) * P].rearrange("p (c n) -> p c n", c=C),
                    cfs[:, CF["vmask"]:CF["vmask"] + HC * HD].unsqueeze(1).to_broadcast([P, C, HC * HD]),
                    ALU.mult).then_inc(s_v4, 1)
            normalise(1)

            def head_max(b, k):
                n = b * TB + k
                dve.wait_ge(s_stok, n + 1)
                nc.vector.tensor_reduce(nm[:, b, k, :], ps[:, STOK[n % 3], :].rearrange("p (h k) -> p h k", h=H),
                                        X, ALU.max, negate=True).then_inc(s_max, 1)

            def split(b):
                dve.wait_ge(s_max, (b + 1) * TB)
                link(nc.vector.tensor_copy(nm2[:, b, :, 0, :], nm[:, b, :, :]))
                nc.vector.tensor_tensor(nm2[:, b, :, 1, :], nm[:, b, :, :], nm2[:, b, :, 0, :],
                                        ALU.subtract).then_inc(s_split, 1)

            def shift_rows(b):
                dve.wait_ge(s_nmt, b + 1)
                nc.vector.tensor_copy(nmt[:, b, :], ps[0:2 * H, 4, b * (T // 2):(b + 1) * (T // 2)].bitcast(BF16)
                                      ).then_inc(s_nmts, 1)

            for k in range(TB):
                head_max(0, k)
            split(0)
            head_max(1, 0)
            head_max(1, 1)
            shift_rows(0)
            head_max(1, 2)
            head_max(1, 3)
            split(1)
            shift_rows(1)

            def tiles(b):
                return slice(b * TB, (b + 1) * TB)

            def own_rank(b):
                dve.wait_ge(s_rank, b + 1)
                return nc.vector.tensor_tensor(mine[:, tiles(b), :], ranks(b), oh[:, tiles(b), :], ALU.mult)

            def whole_rank(b):
                with nc.allow_low_precision("whole numbers below 2^11"):
                    return nc.vector.tensor_reduce(rank[:, tiles(b)], mine[:, tiles(b), :], X, ALU.add)

            def row_of(b):
                return nc.vector.tensor_scalar(low[:, tiles(b)], rank[:, tiles(b)], P - 1, None, ALU.bitwise_and)

            def row_onehot(b):
                nc.vector.tensor_tensor(row_oh[:, tiles(b), :],
                                        cbs[:, CB["lane"]:CB["lane"] + P].unsqueeze(1).to_broadcast([P, TB, P]),
                                        low[:, tiles(b)].unsqueeze(2).to_broadcast([P, TB, P]),
                                        ALU.is_equal).then_inc(s_row_oh, 1)

            def normalise_o(b):
                dve.wait_ge(s_pv, b + 1)
                half = TB * C // 2
                pv = [ps[:, 4 + a, :].rearrange("p (u n) -> p u n", n=64) for a in range(2)]
                link_both(*[nc.vector.reciprocal(rden[:, b, a * half:(a + 1) * half, :], pv[a][:, :, HC * HD:VW])
                            for a in range(2)])
                for a in range(2):
                    nc.vector.tensor_tensor(
                        o[:, b, a * T // 2:(a + 1) * T // 2].rearrange("p (u h d) -> p u h d", h=HC, d=HD),
                        pv[a][:, :, 0:HC * HD].rearrange("p u (h d) -> p u h d", h=HC),
                        rden[:, b, a * half:(a + 1) * half, :].unsqueeze(3).to_broadcast([P, half, HC, HD]),
                        ALU.mult).then_inc(s_o, 1)

            for b in range(B):
                normalise_o(b)
                if b == 1:
                    link(own_rank(0))
                    link(whole_rank(0))
                    link(row_of(0))
                    row_onehot(0)
                t = slice(b * TB, (b + 1) * TB)
                yb = 6 if b == 0 else 2
                ys = ps[:, yb:yb + 2, :].rearrange("p a (t n) -> p (a t) n", t=2)
                dve.wait_ge(s_y, b + 1)
                sc = ys[:, :, D:YW]
                descb = desc.unsqueeze(1).to_broadcast([P, TB, E])

                def stats2(k):
                    return nc.vector.bn_stats(st2[:, b * TB + k, :], ys[:, k, 0:D])
                link_both(nc.vector.tensor_reduce(mx[:, t], sc, X, ALU.max), stats2(0))
                link_both(nc.vector.tensor_tensor(top[:, 0, b, :, :], sc,
                                                  mx[:, t].unsqueeze(2).to_broadcast([P, TB, E]), ALU.is_equal),
                          stats2(1))
                link_both(nc.vector.tensor_tensor(top[:, 1, b, :, :], top[:, 0, b, :, :], descb, ALU.mult), stats2(2))
                link_both(nc.vector.tensor_reduce(mx2[:, t], top[:, 1, b, :, :], X, ALU.max), stats2(3))
                nc.vector.tensor_tensor(oh[:, t, :], descb, mx2[:, t].unsqueeze(2).to_broadcast([P, TB, E]),
                                        ALU.is_equal).then_inc(s_oh, 1)
                for k in range(TB):
                    last = nc.vector.bn_aggr(mv2[:, b * TB + k, :], st2[:, b * TB + k, :])
                link(last)
                nc.vector.tensor_scalar(u2[:, b, 0, :], mv2[:, t, 1], EPS, None, ALU.add)
                nc.vector.tensor_scalar(u2[:, b, 1, :], mv2[:, t, 1], 1.0 + EPS, EPS * EPS, ALU.mult,
                                        ALU.add).then_inc(s_u2, 1)

                def norm2():
                    dve.wait_ge(s_sd2, b + 1)
                    link(nc.vector.reciprocal(r2[:, b, :, :], sd2[:, b, :, :]))
                    nc.vector.scalar_tensor_tensor(nmr[:, b, :], mv2[:, t, 0], -1.0, r2[:, b, 1, :], ALU.mult,
                                                   ALU.mult).then_inc(s_nmr, 1)

                def payload():
                    for k in range(2, TB):
                        last = nc.vector.tensor_scalar(pay[:, b * TB + k, 0:D], ys[:, k, 0:D],
                                                       mv2[:, b * TB + k, 0:1], r2[:, b, 1, k:k + 1],
                                                       ALU.subtract, ALU.mult)
                    last.then_inc(s_zd, 1)
                    nc.vector.scalar_tensor_tensor(pay[:, t, D], r2[:, b, 0, :], 1.0, sd2[:, b, 1, :], ALU.add,
                                                   ALU.mult)
                    nc.vector.tensor_copy(pay[:, t, D + 1], mv2[:, t, 0])
                    nc.vector.tensor_tensor(pay[:, t, D + 2], r2[:, b, 0, :], mx[:, t], ALU.mult).then_inc(s_paya, 1)

                if b == 0:
                    norm2()
                    payload()
            dve.wait_ge(s_rank, 2)
            dve.wait_ge(s_const, 2)
            counts = ps[:, 5, TB * E:(TB + 1) * E]
            link_both(nc.vector.tensor_scalar(cnt[:, 0, :], counts, float(P - 1), None, ALU.add), own_rank(1))
            link_both(nc.vector.tensor_scalar(cnt[:, 1, :], cnt[:, 0, :], -P, None, ALU.bitwise_and), whole_rank(1))
            link_both(nc.vector.tensor_tensor_scan(end[:, 0, :], onesf[:, :], cnt[:, 1, :], 0.0, ALU.mult, ALU.add),
                      row_of(1))
            norm2()
            payload()
            link_both(nc.vector.tensor_tensor(end[:, 1, :], end[:, 0, :], cnt[:, 1, :], ALU.subtract),
                      nc.vector.tensor_scalar(high[:, :], rank[:, :], -P, None, ALU.bitwise_and))
            row_onehot(1)
            link(nc.vector.tensor_tensor(base[:, :, :], oh[:, 0:NT, :],
                                         end[:, 1, :].unsqueeze(1).to_broadcast([P, NT, E]), ALU.mult))
            link(nc.vector.tensor_reduce(first_slot[:, :], base[:, :, :], X, ALU.add))
            link(nc.vector.tensor_tensor(tile[:, :], first_slot[:, :], high[:, :], ALU.add))
            link(nc.vector.tensor_tensor(tile_oh[:, :, :], tile[:, :].unsqueeze(2).to_broadcast([P, NT, NS]),
                                         cfs[:, CF["slot"]:CF["slot"] + NS].unsqueeze(1).to_broadcast([P, NT, NS]),
                                         ALU.is_equal))
            nc.vector.tensor_scalar(tile_code[:, 0, :, :], tile_oh[:, :, :], cfs[:, CF["row"]:CF["row"] + 1], None,
                                    ALU.mult)
            nc.vector.tensor_tensor(tile_code[:, 1, :, :], tile_oh[:, :, :],
                                    cfs[:, CF["code"]:CF["code"] + NT].unsqueeze(2).to_broadcast([P, NT, NS]),
                                    ALU.mult).then_inc(s_tile_oh, 1)
            S1 = NS + 1
            link(nc.vector.tensor_tensor(ge[:, 0, :, :],
                                         cfs[:, CF["slot"]:CF["slot"] + S1].unsqueeze(2).to_broadcast([P, S1, E]),
                                         end[:, 0, :].unsqueeze(1).to_broadcast([P, S1, E]), ALU.is_ge))
            link(nc.vector.tensor_reduce(es[:, 0, :], ge[:, 0, :, :], X, ALU.add))
            link(nc.vector.tensor_scalar(es[:, 1, :], es[:, 0, :], float(E - 1), None, ALU.min))
            nc.vector.tensor_copy(etab[:, :], es[:, 1, :]).then_inc(s_etab, 1)
            dve.wait_ge(s_ids, 1)
            nc.vector.tensor_scalar(idx[:, :], ps[:, 4, 0:NS], float(NOBODY), None, ALU.add).then_inc(s_idx, 1)
            link(nc.vector.tensor_tensor(ge[:, 1, :, :], es[:, 1, :].unsqueeze(2).to_broadcast([P, S1, E]),
                                         cfs[:, CF["expert"]:CF["expert"] + E].unsqueeze(1).to_broadcast([P, S1, E]),
                                         ALU.is_equal))
            for k, name in ((2, "gam"), (3, "bet")):
                link(nc.vector.tensor_tensor(ge[:, k, :, :], ge[:, 1, :, :],
                                             pbs[:, PB[name]:PB[name] + E].unsqueeze(1).to_broadcast([P, S1, E]),
                                             ALU.mult))
                link(nc.vector.tensor_reduce((gsel if k == 2 else bsel)[:, :], ge[:, k, :, :], X, ALU.add))
            dve.wait_ge(s_bcast, 1)
            nc.vector.engine_nop().then_inc(s_zts, CREDIT)
            nc.vector.engine_nop().then_inc(s_hs, CREDIT)
            nc.vector.engine_nop().then_inc(s_fb, CREDIT)

            def scale_shift(n, par):
                dve.wait_ge(s_zt, n + 1)
                nc.vector.tensor_scalar(zts[:, par, :], ps[:, 6 + par, 0:P], gsel[:, bass.ds(n, 1)],
                                        bsel[:, bass.ds(n, 1)], ALU.mult, ALU.add).then_inc(s_zts, 1)

            def add_bias(n, par, e, later=True):
                dve.wait_ge(s_h, n + 1)
                if later:
                    dve.wait_ge(s_hts, n - 1)
                nc.vector.tensor_tensor(hs[:, par, :].rearrange("p (c n) -> p c n", c=FC),
                                        ps[:, par, :].rearrange("p (c n) -> p c n", c=FC),
                                        b1t[:, bass.ds(e, 1), :].rearrange("p a c -> p (a c)").unsqueeze(2)
                                        .to_broadcast([P, FC, P]), ALU.add).then_inc(s_hs, 1)

            def finish(n, par, e):
                dve.wait_ge(s_f, n + 1 + CREDIT)
                nc.vector.tensor_tensor(fb[:, par, :], ps[:, 4 + par, 0:D],
                                        b2b[:, bass.ds(e, 1), :].rearrange("p a n -> p (a n)"),
                                        ALU.add).then_inc(s_fb, 1)
                dve.wait_ge(s_t2, n + 1)
                dve.wait_ge(s_fb, n + 1 + CREDIT)
                nc.vector.scalar_tensor_tensor(fin[:, bass.ds(n, 1), :].rearrange("p a n -> p (a n)"), fb[:, par, :],
                                               alpha[:, bass.ds(n, 1)],
                                               t2[:, bass.ds(n, 1), :].rearrange("p a n -> p (a n)"),
                                               ALU.mult, ALU.add).then_inc(s_fin, 1)

            regs = [dve.alloc_register(name=f"dve_end{k}") for k in range(2 + NS - 12)]
            dve.load(regs[0:2], etab[0:1, 0:2])
            dve.load(regs[2:], etab[0:1, 12:NS])
            e_end = [dve.snap(r, min_val=0, max_val=E - 1) for r in regs]
            scale_shift(0, 0)
            for s in range(2):
                scale_shift(s + 1, (s + 1) % 2)
                add_bias(s, s % 2, e_end[s], later=False)
            regs = [dve.alloc_register(name=f"dve_expert{k}") for k in range(6)]
            with dve.Fori(0, 3) as i:
                dve.load(regs, etab[0:1, bass.ds(i * 4, 6)])
                ee = [dve.snap(r, min_val=0, max_val=E - 1) for r in regs]
                for j in range(4):
                    s = i * 4 + 2 + j
                    scale_shift(s + 1, (j + 1) % 2)
                    add_bias(s, j % 2, ee[j + 2])
                    finish(i * 4 + j, j % 2, ee[j])
            add_bias(NS - 1, (NS - 1) % 2, e_end[4])
            for n in range(12, NS):
                finish(n, n % 2, e_end[n - 12 + 2])

        @block.tensor
        def _(pe):
            mm = nc.tensor.matmul

            def keep_clock_up(bank, times):
                for k in range(times):
                    mm(ps[:, bank, :], filler[:, 0:P], filler[:, :], start=True, stop=True)

            pe.wait_ge(s_filler, 1)
            keep_clock_up(1, 8)
            pe.wait_ge(s_pa, 16)
            mm(ps[:, 4, 0:B * KV], pas[:, 0:P], pas[:, PA["ctx"]:PA["ctx"] + B * KV],
               start=True, stop=True).then_inc(s_kt, 1)
            keep_clock_up(1, 2)
            pe.wait_ge(s_cf, 16)
            pe.wait_ge(s_pb, 16)
            mm(ps[:, 0, 0:E], cfs[:, CF["center"]:CF["center"] + P], pbs[:, PB["cen"]:PB["cen"] + E],
               start=True, stop=True).then_inc(s_cent, 1)

            def fold_keys(b):
                pe.wait_ge(s_kblk, b + 1)
                mm(ps[:, 6 + b, :], pas[:, PA["wq"]:PA["wq"] + P], kblk[:, b, :, :].rearrange("p h k -> p (h k)"),
                   start=True, stop=True).then_inc(s_m, 1)

            def turn_x(b):
                pe.wait_ge(s_xn, b + 1)
                for k in range(TB):
                    last = nc.tensor.transpose(ps[:, 2 + b, k * P:(k + 1) * P], xn[:, b * TB + k, :], ident)
                last.then_inc(s_xnt, 1)

            fold_keys(0)
            turn_x(0)
            pe.wait_ge(s_cents, 1)
            mm(ps[:, 1, 0:E], pbs[:, PB["wo"]:PB["wo"] + P], cfs[:, CF["gap"]:CF["gap"] + E],
               start=True, stop=True).then_inc(s_woc, 1)
            fold_keys(1)
            pe.wait_ge(s_ctx4, 1)
            for b in range(B):
                last = mm(ps[:, 5, b * P:(b + 1) * P], ctx4[:, b, :, :].rearrange("p r k -> p (r k)"),
                          pas[:, PA["wv"]:PA["wv"] + P], start=True, stop=True)
            last.then_inc(s_v4p, 1)

            pe.wait_ge(s_cb, 16)
            causal = cbs[0:KV, CB["causal"]:CB["causal"] + P]

            def scores(b, k):
                n = b * TB + k
                bank = ps[:, STOK[n % 3], :]
                pe.wait_ge(s_ms, b + 1)
                pe.wait_ge(s_xnts, b + 1)
                if n == 1:
                    pe.wait_ge(s_wocs, 1)
                if n == 2:
                    pe.wait_ge(s_v4, B)
                if n >= 3:
                    pe.wait_ge(s_max, n - 2)
                last = mm(bank, xnt[:, n * P:(n + 1) * P], ms[:, b, :], start=True, stop=k > 0)
                if k == 0:
                    last = mm(bank.rearrange("p (c n) -> p c n", c=C), identb[0:KV, :],
                              causal.unsqueeze(1).to_broadcast([KV, C, P]), start=False, stop=True)
                last.then_inc(s_stok, 1)

            def shift_cols(b):
                pe.wait_ge(s_split, b + 1)
                for k in range(TB):
                    c0 = b * (T // 2) + k * 64
                    last = nc.tensor.transpose(ps[0:2 * H, 4, c0:c0 + 64].bitcast(BF16),
                                               nm2[:, b, k, :, :].rearrange("p a h -> p (a h)"), identb)
                last.then_inc(s_nmt, 1)

            def scores_t(b, c):
                n = b * C + c
                if n >= 2:
                    pe.wait_ge(s_exp, n - 1)
                pe.wait_ge(s_nmts, b + 1)
                bank = ps[:, 2 + c % 2, :]
                mm(bank, ms[:, b, c * P:(c + 1) * P], xnt[:, b * T:(b + 1) * T], start=True, stop=False)
                mm(bank[:, 0:KV], causal, identb[0:KV, 0:KV], start=False, stop=False)
                mm(bank, cbs[0:2 * H, CB["spread"] + c * P:CB["spread"] + (c + 1) * P], nmt[:, b, :],
                   start=False, stop=True).then_inc(s_st, 1)

            def weigh(b, c):
                pe.wait_ge(s_exp, b * C + c + 1)
                for k in range(TB):
                    u = k * C + c
                    last = mm(ps[:, 4 + u // 8, (u % 8) * 64:(u % 8) * 64 + VW], pt[:, b, c, k * P:(k + 1) * P],
                              v4[:, b, c, :], start=True, stop=True)
                if c == C - 1:
                    last.then_inc(s_pv, 1)

            def y_of(b, k):
                return ps[:, (6 if b == 0 else 2) + k // 2, (k % 2) * 256:(k % 2) * 256 + YW]

            def residual(b):
                for k in range(TB):
                    mm(y_of(b, k), xts[:, (b * TB + k) * P:(b * TB + k + 1) * P], identc, start=k % 2 == 0,
                       stop=False, skip_group_check=True)

            def turn_o(b):
                if b == 1:
                    pe.wait_ge(s_za, 1)
                    pe.wait_ge(s_zd, 1)
                for k in range(TB):
                    if k % 2 == 0:
                        pe.wait_ge(s_o, b * 2 + k // 2 + 1)
                    last = nc.tensor.transpose(ps[:, OT[b][k // 2], k % 2 * P:(k % 2 + 1) * P], o[:, b, k * P:(k + 1) * P], ident)
                    if k % 2 == 1:
                        last.then_inc(s_ot, 1)

            def project(b):
                for k in range(TB):
                    if k % 2 == 0:
                        pe.wait_ge(s_ots, b * 2 + k // 2 + 1)
                    last = mm(y_of(b, k), ot[:, b, k * P:(k + 1) * P], wo_ext, start=False, stop=True,
                              skip_group_check=True)
                last.then_inc(s_y, 1)

            before = cbs[:, CB["before"]:CB["before"] + P]
            ones = cbs[:, CB["ones"]:CB["ones"] + P]

            def rank_batch_0():
                pe.wait_ge(s_oh, 1)
                out0 = ps[:, 0, 0:TB * E].rearrange("p (t e) -> p t e", e=E)
                last = mm(out0, before, oh[:, 0:TB, :], start=True, stop=False)
                for t in range(TB - 1):
                    last = mm(out0[:, t + 1:, :], ones, oh[:, t:t + 1, :].to_broadcast([P, TB - 1 - t, E]),
                              start=False, stop=t == TB - 2)
                last.then_inc(s_rank, 1)

            ranks1 = ps[:, 5, 0:(TB + 1) * E].rearrange("p (t e) -> p t e", e=E)

            def seed_ranks():
                pe.wait_ge(s_const, 2)
                for t in range(TB):
                    ins = mm(ranks1, ones, oh[:, t:t + 1, :].to_broadcast([P, TB + 1, E]), start=t == 0, stop=False)
                    if t == 0:
                        ins.then_inc(s_f, CREDIT)

            for k in range(3):
                scores(0, k)
            turn_x(1)
            scores(0, 3)
            scores(1, 0)
            scores(1, 1)
            shift_cols(0)
            scores(1, 2)
            scores(1, 3)
            for c in range(C):
                scores_t(0, c)
            shift_cols(1)
            pe.wait_ge(s_xb, 1)
            pe.wait_ge(s_ms, B)
            residual(0)
            pe.wait_ge(s_vones, 1)
            pe.wait_ge(s_nmts, B)
            for c in range(C):
                scores_t(1, c)
                weigh(0, c)
            keep_clock_up(1, 5)
            turn_o(0)
            weigh(1, 0)
            weigh(1, 1)
            project(0)
            weigh(1, 2)
            weigh(1, 3)
            residual(1)
            turn_o(1)
            rank_batch_0()
            seed_ranks()
            project(1)
            pe.wait_ge(s_oh, B)
            mm(ranks1, before, oh[:, TB:, :], start=False, stop=False)
            for t in range(TB, NT):
                last = mm(ranks1[:, t + 1 - TB:, :], ones, oh[:, t:t + 1, :].to_broadcast([P, NT - t, E]),
                          start=False, stop=t == NT - 1)
            last.then_inc(s_rank, 1)
            keep_clock_up(1, 5)
            pe.wait_ge(s_nmr, B)
            keep_clock_up(1, 5)
            pe.wait_ge(s_row_oh, B)
            keep_clock_up(1, 4)
            pe.wait_ge(s_tile_oh, 1)
            for t in range(NT):
                for part in range(2):
                    last = mm(ps[:, 4, 0:NS], row_oh[:, t, :], tile_code[:, part, t, :],
                              start=t + part == 0, stop=t == NT - 1 and part == 1)
            last.then_inc(s_ids, 1)
            keep_clock_up(1, 13)

            def turn(n, par, lane, seen):
                pe.wait_ge(s_zl[lane], seen * 16 + 16)
                pe.wait_ge(s_zts, n + 1)
                nc.tensor.transpose(ps[:, 6 + par, 0:P], zl[:, lane, 0:D], ident).then_inc(s_zt, 1)

            def first(n, par):
                pe.wait_ge(s_w1c, n + 1)
                pe.wait_ge(s_zts, n + 1 + CREDIT)
                pe.wait_ge(s_hs, n + 1)
                for c in range(FC):
                    last = mm(ps[:, par, c * P:(c + 1) * P], w1c[:, par, c * P:(c + 1) * P], zts[:, par, :],
                              start=True, stop=True)
                last.then_inc(s_h, 1)

            def second(n, par, e):
                pe.wait_ge(s_hts, n + 1)
                pe.wait_ge(s_fb, n + 1)
                for c in range(FC):
                    last = mm(ps[:, 4 + par, 0:D], hts[:, par, c * P:(c + 1) * P],
                              w2s[:, bass.ds(e, 1), c * D:(c + 1) * D].rearrange("p a n -> p (a n)"),
                              start=c == 0, stop=c == FC - 1)
                last.then_inc(s_f, 1)

            pe.wait_ge(s_etab, 1)
            pe.wait_ge(s_w2, 16)
            regs = [pe.alloc_register(name=f"pe_end{k}") for k in range(NS - 12)]
            pe.load(regs, etab[0:1, 12:NS])
            e_end = [pe.snap(r, min_val=0, max_val=E - 1) for r in regs]
            turn(0, 0, 0, 0)
            turn(1, 1, 1, 0)
            first(0, 0)
            turn(2, 0, 2, 0)
            first(1, 1)
            regs = [pe.alloc_register(name=f"pe_expert{k}") for k in range(4)]
            with pe.Fori(0, 3) as i:
                pe.load(regs, etab[0:1, bass.ds(i * 4, 4)])
                ee = [pe.snap(r, min_val=0, max_val=E - 1) for r in regs]
                for j in range(4):
                    s = i * 4 + 2 + j
                    turn(s + 1, (j + 1) % 2, (3 + j) % LANES, i + (3 + j) // LANES)
                    first(s, j % 2)
                    second(s - 2, j % 2, ee[j])
            first(NS - 1, 0)
            for n in range(12, NS):
                second(n, n % 2, e_end[n - 12])


def constants():
    import numpy as np
    cf = np.zeros((P, CF_W), np.float32)
    r = np.arange(P)
    cf[:, CF["ident"]:CF["ident"] + P] = np.eye(P)
    cf[:, CF["center"]:CF["center"] + P] = np.eye(P) - 1.0 / D
    cf[:, CF["hmask"]:CF["hmask"] + H] = r[:, None] // HD == np.arange(H)[None]
    cf[:, CF["vmask"]:CF["vmask"] + HC * HD] = r[:, None] // KV == np.arange(HC * HD)[None] // HD
    cf[:, CF["ones"]:CF["ones"] + HC] = r[:, None] // KV == np.arange(HC)[None]
    cf[:, CF["desc"]:CF["desc"] + E] = E - np.arange(E)[None]
    cf[:, CF["code"]:CF["code"] + NT] = P * np.arange(NT)[None] - NOBODY
    cf[:, CF["row"]] = r
    cf[:, CF["expert"]:CF["expert"] + E] = np.arange(E)[None]
    cf[:, CF["slot"]:CF["slot"] + NS + 1] = P * np.arange(NS + 1)[None]
    cb = np.zeros((P, CB_W), np.float32)
    cb[:, CB["ident"]:CB["ident"] + P] = np.eye(P)
    cb[:, CB["before"]:CB["before"] + P] = r[:, None] < r[None]
    cb[:, CB["ones"]:CB["ones"] + P] = 1.0
    rows = np.arange(2 * H)[:, None] % H
    cb[0:2 * H, CB["spread"]:CB["spread"] + C * P] = rows == np.arange(C * P)[None] // KV
    cb[0:KV, CB["causal"]:CB["causal"] + P] = np.where(np.arange(P)[None] % KV > np.arange(KV)[:, None], NEG, 0.0)
    cb[:, CB["lane"]:CB["lane"] + P] = r[None]
    return cf, (cb.view(np.uint32) >> 16).astype(np.uint16)


def kernel(x, ctx_1024, L0_xattn_Wq, L0_xattn_Wk, L0_xattn_Wv, L0_xattn_Wo, L0_xattn_bo, L0_ffn_centroids,
           L0_ffn_gamma, L0_ffn_beta, L0_ffn_W1, L0_ffn_b1, L0_ffn_W2, L0_ffn_b2):
    import numpy as np
    import concourse.bacc as bacc
    from concourse import mybir as mb
    from concourse.bass_utils import run_bass_kernel_spmd as run

    def a(v):
        return np.asarray(v)
    cf, cb = constants()
    arrays = {
        "x": np.ascontiguousarray(a(x)),
        "xt": np.ascontiguousarray(a(x).reshape(B * T, D).T),
        "pa": np.ascontiguousarray(np.concatenate([
            a(L0_xattn_Wk).T, a(ctx_1024).reshape(B * KV, D).T, a(L0_xattn_Wv).T, a(L0_xattn_Wq)], axis=1)),
        "pb": np.ascontiguousarray(np.concatenate([
            a(L0_xattn_Wo), a(L0_xattn_Wo).T, a(L0_ffn_centroids).T, a(L0_ffn_gamma).T, a(L0_ffn_beta).T,
            a(L0_ffn_b1).reshape(E * FC, P).T, a(L0_xattn_bo)[:, None]], axis=1)),
        "cf": cf,
        "cb": cb,
        "b2": np.ascontiguousarray(a(L0_ffn_b2).reshape(1, -1)),
        "w1": np.ascontiguousarray(a(L0_ffn_W1).transpose(2, 0, 1)),
        "w2": np.ascontiguousarray(a(L0_ffn_W2).reshape(E, D, FC, P).transpose(3, 0, 2, 1).reshape(P, E, FC * D)),
    }
    nc = bacc.Bacc("TRN2", target_bir_lowering=False, num_devices=1)
    aps = [nc.dram_tensor(f"in_{k}", v.shape, mb.dt.from_np(v.dtype), kind="ExternalInput").ap()
           for k, v in arrays.items()]
    out = nc.dram_tensor("out", (B, T, D), mb.dt.float32, kind="ExternalOutput").ap()
    xattn_moe(nc, *aps, out)
    r = run(nc, [{f"in_{k}": v for k, v in arrays.items()}], core_ids=[0])
    return r.results[0]["out"]
```

```python
from contextlib import ExitStack

import concourse.bass as bass
from concourse import mybir

F32 = mybir.dt.float32
BF16 = mybir.dt.bfloat16
F32R = mybir.dt.float32r
I32 = mybir.dt.int32
ALU = mybir.AluOpType
ACT = mybir.ActivationFunctionType
X = mybir.AxisListType.X

P = 128
B, T, D = 2, 512, 128
TB = T // P
NT = B * TB
KV = 32
H, HD = 16, 8
HC = P // KV
C = H // HC
E, F = 8, 512
FC = F // P
EPS = 1e-5
SCALE = float(HD) ** -0.5
NEG = -1e37
NS = NT + E - 1
ROW = D + 3
LANES = 6
LOOPS = (NS - 3) // LANES
TAIL = LOOPS * LANES
VW = HC * HD + HC
PV = (4, 5), (0, 1)
OT = (4, 5), (0, 1)
YW = D + E
STOK = (0, 1, 5)
NOBODY = 4096

PA = dict(wk=0, ctx=128, wv=192, wq=320)
PA_W = 448
PB = dict(wo=0, wot=128, cen=256, gam=264, bet=272, b1=280, bo=312)
PB_W = 313
CF = dict(ident=0, gap=128, center=136, hmask=264, vmask=280, ones=312, desc=316, code=324, expert=332, slot=340, row=356)
CF_W = 357
CB = dict(ident=0, before=128, ones=256, spread=384, causal=896, lane=1024)
CB_W = 1152


def xattn_moe(nc, x, xt, pa, pb, cf, cb, b2, w1, w2, out):
    rows = nc.dram_tensor("token_rows", [B * T, ROW], F32, kind="Internal").ap()
    row_tiles = rows.rearrange("(b t p) d -> b p t d", b=B, p=P)
    out_rows = out.rearrange("b t d -> (b t) d")
    x_tiles = x.rearrange("b (t p) d -> b p t d", p=P)
    ctx = ExitStack()
    with ctx:
        def sb(name, shape, dt=F32):
            return ctx.enter_context(nc.sbuf_tensor(name, shape, dt))

        def sem(name):
            return ctx.enter_context(nc.semaphore(name))

        xs = sb("xs", [P, NT, D])
        xts = sb("xts", [P, NT * P])
        pas = sb("pas", [P, PA_W])
        pbs = sb("pbs", [P, PB_W])
        cfs = sb("cfs", [P, CF_W])
        cbw = sb("cbw", [P, CB_W], mybir.dt.uint16)
        cbs = cbw[:, :].bitcast(BF16)
        b2s = sb("b2s", [1, E * D])
        w1s = sb("w1s", [P, E, F])
        w2s = sb("w2s", [P, E, FC * D])
        b2b = sb("b2b", [P, E, D])
        b1t = pbs[:, PB["b1"]:PB["b1"] + E * FC].rearrange("p (e c) -> p e c", e=E)
        ident = cfs[:, 0:P]
        identb = cbs[:, 0:P]
        identc = cfs[:, 0:YW]
        wo_ext = pbs[:, PB["wot"]:PB["wot"] + YW]
        desc = cfs[:, CF["desc"]:CF["desc"] + E]
        kblk = sb("kblk", [P, B, H, KV])
        ctx4 = sb("ctx4", [P, B, HC, KV])
        v4 = sb("v4", [P, B, C, VW])
        ms = sb("ms", [P, B, H * KV])
        st = sb("st", [P, NT, 6])
        mv = sb("mv", [P, NT, 2])
        ve = sb("ve", [P, NT])
        sd = sb("sd", [P, NT])
        rs = sb("rs", [P, NT])
        filler = sb("filler", [P, 512], BF16)
        tiny = sb("tiny", [P, 4])
        xn = sb("xn", [P, NT, D])
        xnt = sb("xnt", [P, NT * P])
        msr = sb("msr", [P, B, 2, H * KV], F32R)
        xntr = sb("xntr", [P, B, 2, T], F32R)
        nm = sb("nm", [P, B, TB, H])
        nm2 = sb("nm2", [P, B, TB, 2, H], BF16)
        nmt = sb("nmt", [2 * H, B, T], BF16)
        pt = sb("pt", [P, B, C, T])
        rden = sb("rden", [P, B, TB * C, HC])
        o = sb("o", [P, B, T])
        ot = sb("ot", [P, B, T])
        st2 = sb("st2", [P, NT, 6])
        mv2 = sb("mv2", [P, NT, 2])
        u2 = sb("u2", [P, B, 2, TB])
        sd2 = sb("sd2", [P, B, 2, TB])
        r2 = sb("r2", [P, B, 2, TB])
        ratio = sb("ratio", [P, NT])
        nmr = sb("nmr", [P, B, TB])
        mx = sb("mx", [P, NT])
        top = sb("top", [P, 3, B, TB, E])
        mx2 = sb("mx2", [P, NT])
        oh = sb("oh", [P, NT + 1, E], BF16)
        pay = sb("pay", [P, NT, ROW])
        cnt = sb("cnt", [P, 2, E], I32)
        onesf = sb("onesf", [P, E])
        end = sb("end", [P, 2, E])
        mine = sb("mine", [P, NT, E])
        rank = sb("rank", [P, NT], I32)
        low = sb("low", [P, NT], I32)
        lowb = sb("lowb", [P, NT], BF16)
        high = sb("high", [P, NT], I32)
        row_oh = sb("row_oh", [P, NT, P], BF16)
        base = sb("base", [P, NT, E])
        first_slot = sb("first_slot", [P, NT])
        tile = sb("tile", [P, NT])
        tile_oh = sb("tile_oh", [P, NT, NS])
        tile_code = sb("tile_code", [P, NT, 2, NS], BF16)
        code_sums = sb("code_sums", [P, 2 * NS])
        idx = sb("idx", [P, NS], I32)
        ge = sb("ge", [P, 5, NS + 1, E])
        es = sb("es", [P, 2, NS + 1])
        etab = sb("etab", [P, NS + 1], I32)
        gsel = sb("gsel", [P, NS + 1])
        bsel = sb("bsel", [P, NS + 1])
        zl = sb("zl", [P, LANES, ROW])
        zts = sb("zts", [P, 2, P])
        w1c = sb("w1c", [P, 2, F])
        hs = sb("hs", [P, 2, F])
        hts = sb("hts", [P, 2, F])
        t2 = sb("t2", [P, NS, D])
        alpha = sb("alpha", [P, NS])
        fb = sb("fb", [P, 2, D])
        fin = sb("fin", [P, NS, D])

        ps = ctx.enter_context(nc.psum_tensor("ps", [P, 8, 512], F32))

        def sems(names):
            return [sem(n) for n in names.split()]

        s_x = [sem(f"s_x{b}") for b in range(B)]
        s_pa, s_pb, s_cf, s_cb, s_xt, s_b2, s_w1, s_w2 = sems("s_pa s_pb s_cf s_cb s_xt s_b2 s_w1 s_w2")
        s_filler = sem("s_filler")
        s_blank, s_const, s_bcast, s_ctx4, s_kt, s_kblk, s_v4p, s_v4, s_vones = sems(
            "s_blank s_const s_bcast s_ctx4 s_kt s_kblk s_v4p s_v4 s_vones")
        s_cent, s_cents, s_woc, s_wocs, s_m, s_ms, s_xb, s_high, s_low = sems("s_cent s_cents s_woc s_wocs s_m s_ms s_xb s_high s_low")
        s_ve, s_sd, s_xn, s_xnt, s_xnts = sems("s_ve s_sd s_xn s_xnt s_xnts")
        s_stok, s_max, s_split, s_nmt, s_nmts = sems("s_stok s_max s_split s_nmt s_nmts")
        s_st, s_exp, s_pv, s_o, s_ot, s_ots, s_y = sems("s_st s_exp s_pv s_o s_ot s_ots s_y")
        s_oh, s_u2, s_sd2, s_nmr, s_paya, s_za, s_zd, s_rank, s_row_oh, s_tile_oh, s_ids, s_idx, s_etab, s_written = sems(
            "s_oh s_u2 s_sd2 s_nmr s_paya s_za s_zd s_rank s_row_oh s_tile_oh s_ids s_idx s_etab s_written")
        s_zl = [sem(f"s_zl{j}") for j in range(LANES)]
        s_zt, s_zts, s_w1c, s_h, s_hs, s_hts, s_f, s_fb, s_fin, s_t2, s_out = sems(
            "s_zt s_zts s_w1c s_h s_hs s_hts s_f s_fb s_fin s_t2 s_out")
        s_dve, s_pool = sems("s_dve s_pool")
        CREDIT = 2

        block = ctx.enter_context(nc.Block())

        @block.sync
        def _(sp):
            sp.dma_start(xs[:, 0:TB, :], x_tiles[0]).then_inc(s_x[0], 16)
            sp.dma_start(cfs[:, :], cf).then_inc(s_cf, 16)
            sp.dma_start(xs[:, TB:, :], x_tiles[1]).then_inc(s_x[1], 16)
            sp.dma_start(pbs[:, :], pb).then_inc(s_pb, 16)
            sp.dma_start(xts[:, :], xt).then_inc(s_xt, 16)
            sp.dma_start(cbw[:, :], cb).then_inc(s_cb, 16)
            sp.dma_start(b2s[:, :], b2).then_inc(s_b2, 16)
            sp.dma_start(w1s[:, :, :], w1).then_inc(s_w1, 16)
            sp.dma_start(w2s[:, :, :], w2).then_inc(s_w2, 16)
            for b in range(B):
                sp.wait_ge(s_paya, b + 1)
                sp.wait_ge(s_za, b + 1)
                if b == 1:
                    sp.wait_ge(s_zd, 1)
                sp.dma_start(row_tiles[b], pay[:, b * TB:(b + 1) * TB, :]).then_inc(s_written, 16)

        @block.gpsimd
        def _(pool):
            nc.gpsimd.memset(tiny[:, :], 1.0).then_inc(s_const, 1)
            nc.gpsimd.memset(oh[:, NT, :], 0.0)
            nc.gpsimd.memset(onesf[:, :], 1.0).then_inc(s_const, 1)
            pool.wait_ge(s_cf, 16)
            nc.gpsimd.tensor_copy(v4[:, :, :, HC * HD:].rearrange("p b c h -> p (b c) h"),
                                  cfs[:, CF["ones"]:CF["ones"] + HC].unsqueeze(1).to_broadcast([P, B * C, HC])
                                  ).then_inc(s_vones, 1)
            nc.gpsimd.memset(zl[:, :, :], 0.0).then_inc(s_blank, 1)
            pool.wait_ge(s_b2, 16)
            nc.gpsimd.partition_broadcast(b2b[:, :, :].rearrange("p e d -> p (e d)"), b2s[0:1, :],
                                          channels=P).then_inc(s_bcast, 1)
            for k, (whole, parts, b) in enumerate(((ms[:, 0, :], msr, 0), (xnt[:, 0:T], xntr, 0),
                                                   (ms[:, 1, :], msr, 1), (xnt[:, T:], xntr, 1))):
                pool.wait_ge(s_high, k + 1)
                nc.gpsimd.tensor_tensor(parts[:, b, 1, :], whole, parts[:, b, 0, :].bitcast(F32),
                                        ALU.subtract).then_inc(s_low, 1)
            for b in range(B):
                t = slice(b * TB, (b + 1) * TB)
                pool.wait_ge(s_nmr, b + 1)
                nc.gpsimd.tensor_tensor(ratio[:, t], r2[:, b, 0, :], sd2[:, b, 1, :], ALU.mult).then_inc(s_pool, 1)
                nc.gpsimd.tensor_copy(pay[:, t, D + 1], mv2[:, t, 0])
                nc.gpsimd.tensor_tensor(pay[:, t, D + 2], r2[:, b, 0, :], mx[:, t], ALU.mult)
                pool.wait_ge(s_pool, b + 1)
                nc.gpsimd.tensor_tensor(pay[:, t, D], ratio[:, t], sd2[:, b, 1, :], ALU.add).then_inc(s_paya, 1)
            pool.wait_ge(s_blank, 1)
            pool.wait_ge(s_idx, 1)
            pool.wait_ge(s_written, 16 * B)

            def gather(n):
                if n >= LANES:
                    pool.wait_ge(s_zl[n % LANES], 16 * (n // LANES))
                    pool.wait_ge(s_zt, n - LANES + 1)
                    pool.wait_ge(s_t2, n - LANES + 1)
                nc.gpsimd.indirect_dma_start(
                    out=zl[:, n % LANES, :], out_offset=None,
                    in_=rows, in_offset=bass.IndirectOffsetOnAxis(ap=idx[:, n:n + 1], axis=0),
                    bounds_check=B * T - 1, oob_is_err=False).then_inc(s_zl[n % LANES], 16)

            def send(n):
                pool.wait_ge(s_fin, n + 1)
                nc.gpsimd.indirect_dma_start(
                    out=out_rows, out_offset=bass.IndirectOffsetOnAxis(ap=idx[:, n:n + 1], axis=0),
                    in_=fin[:, n, :], in_offset=None, bounds_check=B * T - 1, oob_is_err=False).then_inc(s_out, 16)

            for n in range(NS + LANES + 2):
                if n < NS:
                    gather(n)
                if n >= LANES + 2:
                    send(n - LANES - 2)
            pool.wait_ge(s_out, 16 * NS)

        @block.scalar
        def _(act):
            act.dma_start(pas[:, :], pa).then_inc(s_pa, 16)
            act.wait_ge(s_const, 1)
            nc.scalar.activation(tiny[:, 1:2], tiny[:, 0:1], ACT.Sqrt)
            act.wait_ge(s_pa, 16)
            for b in range(B):
                c0 = PA["ctx"] + b * KV
                last = nc.scalar.copy(ctx4[:, b, :, :],
                                      pas[:, c0:c0 + KV].unsqueeze(1).to_broadcast([P, HC, KV]))
            last.then_inc(s_ctx4, 1)

            def std(b):
                act.wait_ge(s_ve, b + 1)
                t = slice(b * TB, (b + 1) * TB)
                nc.scalar.activation(sd[:, t], ve[:, t], ACT.Sqrt).then_inc(s_sd, 1)

            std(0)
            act.wait_ge(s_cent, 1)
            nc.scalar.copy(cfs[:, CF["gap"]:CF["gap"] + E], ps[:, 0, 0:E]).then_inc(s_cents, 1)
            act.wait_ge(s_m, 1)
            nc.scalar.copy(ms[:, 0, :], ps[:, 6, :]).then_inc(s_ms, 1)
            act.wait_ge(s_xnt, 1)
            nc.scalar.copy(xnt[:, 0:T], ps[:, 2, :]).then_inc(s_xnts, 1)
            act.wait_ge(s_woc, 1)
            nc.scalar.copy(pbs[:, PB["cen"]:PB["cen"] + E], ps[:, 1, 0:E]).then_inc(s_wocs, 1)
            std(1)
            act.wait_ge(s_m, 2)
            nc.scalar.copy(ms[:, 1, :], ps[:, 7, :]).then_inc(s_ms, 1)
            def high_part(which, b):
                src, parts = (ms[:, b, :], msr) if which == "ms" else (xnt[:, b * T:(b + 1) * T], xntr)
                nc.scalar.copy(parts[:, b, 0, :], src).then_inc(s_high, 1)

            act.wait_ge(s_ms, B)
            act.wait_ge(s_xnts, 1)
            high_part("ms", 0)
            high_part("xnt", 0)
            high_part("ms", 1)
            act.wait_ge(s_xnt, 2)
            nc.scalar.copy(xnt[:, T:], ps[:, 3, :]).then_inc(s_xnts, 1)
            act.wait_ge(s_xnts, 2)
            high_part("xnt", 1)
            act.wait_ge(s_xt, 16)
            act.wait_ge(s_pb, 16)
            nc.scalar.activation(xts[:, :], xts[:, :], ACT.Identity, bias=pbs[:, PB["bo"]:PB["bo"] + 1]
                                 ).then_inc(s_xb, 1)
            nc.scalar.activation(tiny[:, 2:3], tiny[:, 0:1], ACT.Exp)
            for b in range(B):
                for c in range(C):
                    act.wait_ge(s_st, b * C + c + 1)
                    nc.scalar.activation(pt[:, b, c, :], ps[:, 2 + c % 2, :], ACT.Exp, scale=SCALE).then_inc(s_exp, 1)
            nc.scalar.activation(tiny[:, 1:2], tiny[:, 0:1], ACT.Sqrt)

            def copy_ot(b):
                for a in range(2):
                    act.wait_ge(s_ot, b * 2 + a + 1)
                    h = slice(a * T // 2, (a + 1) * T // 2)
                    nc.scalar.copy(ot[:, b, h], ps[:, OT[b][a], 0:T // 2]).then_inc(s_ots, 1)

            def std2(b):
                act.wait_ge(s_u2, b + 1)
                nc.scalar.activation(sd2[:, b, :, :], u2[:, b, :, :], ACT.Sqrt).then_inc(s_sd2, 1)

            def make_z(b):
                act.wait_ge(s_nmr, b + 1)
                for k in range(TB if b == 0 else 2):
                    last = nc.scalar.activation(pay[:, b * TB + k, 0:D],
                                                ps[:, (6 if b == 0 else 2) + k // 2, k % 2 * 256:k % 2 * 256 + D],
                                                ACT.Identity, scale=r2[:, b, 1, k:k + 1], bias=nmr[:, b, k:k + 1])
                last.then_inc(s_za, 1)

            copy_ot(0)
            copy_ot(1)
            std2(0)
            make_z(0)
            std2(1)
            make_z(1)
            nc.scalar.activation(tiny[:, 3:4], tiny[:, 0:1], ACT.Sigmoid)
            act.wait_ge(s_etab, 1)
            act.wait_ge(s_w1, 16)

            def stage(n, par, lane, seen, e, later=True):
                if later:
                    act.wait_ge(s_h, n - 1)
                nc.scalar.copy(w1c[:, par, :], w1s[:, bass.ds(e, 1), :].rearrange("p a n -> p (a n)")
                               ).then_inc(s_w1c, 1)
                act.wait_ge(s_zl[lane], seen * 16 + 16)
                zrow = zl[:, lane, :]
                nc.scalar.activation(alpha[:, bass.ds(n, 1)], zrow[:, D + 2:D + 3], ACT.Sigmoid)
                nc.scalar.activation(t2[:, bass.ds(n, 1), :].rearrange("p a n -> p (a n)"), zrow[:, 0:D], ACT.Identity,
                                     scale=zrow[:, D:D + 1], bias=zrow[:, D + 1:D + 2]).then_inc(s_t2, 1)

            def relu(n, par):
                act.wait_ge(s_hs, n + 1 + CREDIT)
                act.wait_ge(s_f, n + 1)
                nc.scalar.activation(hts[:, par, :], hs[:, par, :], ACT.Relu).then_inc(s_hts, 1)

            regs = [act.alloc_register(name=f"act_end{k}") for k in range(3)]
            act.load(regs[0:2], etab[0:1, 0:2])
            act.load(regs[2:3], etab[0:1, NS - 1:NS])
            e_end = [act.snap(r, min_val=0, max_val=E - 1) for r in regs]
            for n in range(2):
                stage(n, n, n, 0, e_end[n], later=False)
            regs = [act.alloc_register(name=f"act_expert{k}") for k in range(LANES)]
            with act.Fori(0, LOOPS) as i:
                act.load(regs, etab[0:1, bass.ds(i * LANES + 2, LANES)])
                ee = [act.snap(r, min_val=0, max_val=E - 1) for r in regs]
                for j in range(LANES):
                    stage(i * LANES + 2 + j, j % 2, (2 + j) % LANES, i + (2 + j) // LANES, ee[j])
                    relu(i * LANES + j, j % 2)
            stage(NS - 1, 0, (NS - 1) % LANES, (NS - 1) // LANES, e_end[2])
            for n in range(TAIL, NS):
                relu(n, n % 2)

        @block.vector
        def _(dve):
            chain = [0]

            def ranks(b):
                return ps[:, 4 + b, 0:TB * E].rearrange("p (t e) -> p t e", e=E)

            def link(ins, meanwhile=None):
                chain[0] += 1
                ins.then_inc(s_dve, 1)
                if meanwhile:
                    meanwhile()
                dve.wait_ge(s_dve, chain[0])

            def link_all(*all_ins, meanwhile=None):
                for ins in all_ins:
                    ins.then_inc(s_dve, 1)
                chain[0] += len(all_ins)
                if meanwhile:
                    meanwhile()
                dve.wait_ge(s_dve, chain[0])

            def stats(b):
                dve.wait_ge(s_x[b], 16)
                for t in range(b * TB, (b + 1) * TB):
                    last = nc.vector.bn_stats(st[:, t, :], xs[:, t, :])
                link(last)
                for t in range(b * TB, (b + 1) * TB):
                    last = nc.vector.bn_aggr(mv[:, t, :], st[:, t, :])
                link(last)
                t = slice(b * TB, (b + 1) * TB)
                nc.vector.tensor_scalar(ve[:, t], mv[:, t, 1], EPS, None, ALU.add).then_inc(s_ve, 1)

            def normalise(b):
                dve.wait_ge(s_sd, b + 1)
                link(nc.vector.reciprocal(rs[:, b * TB:(b + 1) * TB], sd[:, b * TB:(b + 1) * TB]))
                for t in range(b * TB, (b + 1) * TB):
                    last = nc.vector.tensor_scalar(xn[:, t, :], xs[:, t, :], mv[:, t, 0:1], rs[:, t:t + 1],
                                                   ALU.subtract, ALU.mult)
                last.then_inc(s_xn, 1)

            def spread_keys(b):
                nc.vector.tensor_tensor(
                    kblk[:, b, :, :], ps[:, 4, b * KV:(b + 1) * KV].unsqueeze(1).to_broadcast([P, H, KV]),
                    cfs[:, CF["hmask"]:CF["hmask"] + H].unsqueeze(2).to_broadcast([P, H, KV]),
                    ALU.mult).then_inc(s_kblk, 1)

            nc.vector.memset(filler[:, :], 0.0).then_inc(s_filler, 1)
            stats(0)
            dve.wait_ge(s_cf, 16)
            dve.wait_ge(s_kt, 1)
            spread_keys(0)
            normalise(0)
            spread_keys(1)
            stats(1)
            dve.wait_ge(s_v4p, 1)
            for b in range(B):
                nc.vector.tensor_tensor(
                    v4[:, b, :, 0:HC * HD], ps[:, 5, b * P:(b + 1) * P].rearrange("p (c n) -> p c n", c=C),
                    cfs[:, CF["vmask"]:CF["vmask"] + HC * HD].unsqueeze(1).to_broadcast([P, C, HC * HD]),
                    ALU.mult).then_inc(s_v4, 1)
            normalise(1)

            def head_max(b, k):
                n = b * TB + k
                dve.wait_ge(s_stok, n + 1)
                nc.vector.tensor_reduce(nm[:, b, k, :], ps[:, STOK[n % 3], :].rearrange("p (h k) -> p h k", h=H),
                                        X, ALU.max, negate=True).then_inc(s_max, 1)

            def split(b):
                dve.wait_ge(s_max, (b + 1) * TB)
                link(nc.vector.tensor_copy(nm2[:, b, :, 0, :], nm[:, b, :, :]))
                nc.vector.tensor_tensor(nm2[:, b, :, 1, :], nm[:, b, :, :], nm2[:, b, :, 0, :],
                                        ALU.subtract).then_inc(s_split, 1)

            def shift_rows(b):
                dve.wait_ge(s_nmt, b + 1)
                nc.vector.tensor_copy(nmt[:, b, :], ps[0:2 * H, 4, b * (T // 2):(b + 1) * (T // 2)].bitcast(BF16)
                                      ).then_inc(s_nmts, 1)

            for k in range(TB):
                head_max(0, k)
            split(0)
            head_max(1, 0)
            head_max(1, 1)
            shift_rows(0)
            head_max(1, 2)
            head_max(1, 3)
            split(1)
            shift_rows(1)

            def tiles(b):
                return slice(b * TB, (b + 1) * TB)

            def own_rank(b):
                dve.wait_ge(s_rank, b + 1)
                return nc.vector.tensor_tensor(mine[:, tiles(b), :], ranks(b), oh[:, tiles(b), :], ALU.mult)

            def whole_rank(b):
                with nc.allow_low_precision("whole numbers below 2^11"):
                    return nc.vector.tensor_reduce(rank[:, tiles(b)], mine[:, tiles(b), :], X, ALU.add)

            def row_of(b):
                return nc.vector.tensor_scalar(low[:, tiles(b)], rank[:, tiles(b)], P - 1, None, ALU.bitwise_and)

            def low_rank(b):
                return nc.vector.tensor_copy(lowb[:, tiles(b)], low[:, tiles(b)])

            def row_onehot(n):
                return nc.vector.tensor_tensor(row_oh[:, n, :], cbs[:, CB["lane"]:CB["lane"] + P],
                                               lowb[:, n:n + 1].to_broadcast([P, P]), ALU.is_equal
                                               ).then_inc(s_row_oh, 1)

            def normalise_o(b):
                half = TB * C // 2
                pv = [ps[:, PV[b][a], :].rearrange("p (u n) -> p u n", n=64) for a in range(2)]
                both = []
                for a in range(2):
                    dve.wait_ge(s_pv, b * 2 + a + 1)
                    both.append(nc.vector.reciprocal(rden[:, b, a * half:(a + 1) * half, :], pv[a][:, :, HC * HD:VW]))
                link_all(*both)
                for a in range(2):
                    nc.vector.tensor_tensor(
                        o[:, b, a * T // 2:(a + 1) * T // 2].rearrange("p (u h d) -> p u h d", h=HC, d=HD),
                        pv[a][:, :, 0:HC * HD].rearrange("p u (h d) -> p u h d", h=HC),
                        rden[:, b, a * half:(a + 1) * half, :].unsqueeze(3).to_broadcast([P, half, HC, HD]),
                        ALU.mult).then_inc(s_o, 1)

            normalise_o(0)
            normalise_o(1)
            for b in range(B):
                t = tiles(b)
                yb = 6 if b == 0 else 2
                ys = ps[:, yb:yb + 2, :].rearrange("p a (t n) -> p (a t) n", t=2)
                sc = ys[:, :, D:YW]
                descb = desc.unsqueeze(1).to_broadcast([P, TB, E])

                def stats2(k):
                    return nc.vector.bn_stats(st2[:, b * TB + k, :], ys[:, k, 0:D])
                ranks0 = [own_rank, whole_rank, row_of, low_rank] if b == 1 else []

                def beside(step):
                    return [ranks0[step](0)] if ranks0 else []
                dve.wait_ge(s_y, b * 2 + 1)
                two = [stats2(0), stats2(1)]
                dve.wait_ge(s_y, b * 2 + 2)
                link_all(nc.vector.tensor_reduce(mx[:, t], sc, X, ALU.max), *two, stats2(2), *beside(0))
                link_all(nc.vector.tensor_tensor(top[:, 0, b, :, :], sc,
                                                 mx[:, t].unsqueeze(2).to_broadcast([P, TB, E]), ALU.is_equal),
                         stats2(3), *beside(1))
                link_all(nc.vector.tensor_tensor(top[:, 1, b, :, :], top[:, 0, b, :, :], descb, ALU.mult),
                         *[nc.vector.bn_aggr(mv2[:, b * TB + k, :], st2[:, b * TB + k, :]) for k in range(TB)],
                         *beside(2))
                nc.vector.tensor_scalar(u2[:, b, 0, :], mv2[:, t, 1], EPS, None, ALU.add)
                nc.vector.tensor_scalar(u2[:, b, 1, :], mv2[:, t, 1], 1.0 + EPS, EPS * EPS, ALU.mult,
                                        ALU.add).then_inc(s_u2, 1)
                link_all(nc.vector.tensor_reduce(mx2[:, t], top[:, 1, b, :, :], X, ALU.max), *beside(3))
                nc.vector.tensor_tensor(oh[:, t, :], descb, mx2[:, t].unsqueeze(2).to_broadcast([P, TB, E]),
                                        ALU.is_equal).then_inc(s_oh, 1)
                if b == 1:
                    row_onehot(0)
                dve.wait_ge(s_sd2, b + 1)
                link(nc.vector.reciprocal(r2[:, b, :, :], sd2[:, b, :, :]))
                nc.vector.scalar_tensor_tensor(nmr[:, b, :], mv2[:, t, 0], -1.0, r2[:, b, 1, :], ALU.mult,
                                               ALU.mult).then_inc(s_nmr, 1)
            for k in range(2, TB):
                last = nc.vector.tensor_scalar(pay[:, TB + k, 0:D], ys[:, k, 0:D], mv2[:, TB + k, 0:1],
                                               r2[:, 1, 1, k:k + 1], ALU.subtract, ALU.mult)
            last.then_inc(s_zd, 1)
            dve.wait_ge(s_rank, 2)
            dve.wait_ge(s_const, 2)
            counts = ps[:, 5, TB * E:(TB + 1) * E]
            link_all(nc.vector.tensor_scalar(cnt[:, 0, :], counts, float(P - 1), None, ALU.add), own_rank(1),
                     meanwhile=lambda: row_onehot(1))
            link_all(nc.vector.tensor_scalar(cnt[:, 1, :], cnt[:, 0, :], -P, None, ALU.bitwise_and), whole_rank(1),
                     meanwhile=lambda: row_onehot(2))
            link_all(nc.vector.tensor_tensor_scan(end[:, 0, :], onesf[:, :], cnt[:, 1, :], 0.0, ALU.mult, ALU.add),
                     row_of(1), meanwhile=lambda: row_onehot(3))
            link_all(nc.vector.tensor_tensor(end[:, 1, :], end[:, 0, :], cnt[:, 1, :], ALU.subtract),
                     low_rank(1),
                     nc.vector.tensor_scalar(high[:, :], rank[:, :], -P, None, ALU.bitwise_and))
            link(nc.vector.tensor_tensor(base[:, :, :], oh[:, 0:NT, :],
                                         end[:, 1, :].unsqueeze(1).to_broadcast([P, NT, E]), ALU.mult),
                 lambda: row_onehot(TB))
            link(nc.vector.tensor_reduce(first_slot[:, :], base[:, :, :], X, ALU.add),
                 lambda: row_onehot(TB + 1))
            link(nc.vector.tensor_tensor(tile[:, :], first_slot[:, :], high[:, :], ALU.add),
                 lambda: row_onehot(TB + 2))
            link(nc.vector.tensor_tensor(tile_oh[:, :, :], tile[:, :].unsqueeze(2).to_broadcast([P, NT, NS]),
                                         cfs[:, CF["slot"]:CF["slot"] + NS].unsqueeze(1).to_broadcast([P, NT, NS]),
                                         ALU.is_equal),
                 lambda: row_onehot(TB + 3))
            nc.vector.tensor_scalar(tile_code[:, :, 0, :], tile_oh[:, :, :], cfs[:, CF["row"]:CF["row"] + 1], None,
                                    ALU.mult)
            nc.vector.tensor_tensor(tile_code[:, :, 1, :], tile_oh[:, :, :],
                                    cfs[:, CF["code"]:CF["code"] + NT].unsqueeze(2).to_broadcast([P, NT, NS]),
                                    ALU.mult).then_inc(s_tile_oh, 1)
            S1 = NS + 1
            link(nc.vector.tensor_tensor(ge[:, 0, :, :],
                                         cfs[:, CF["slot"]:CF["slot"] + S1].unsqueeze(2).to_broadcast([P, S1, E]),
                                         end[:, 0, :].unsqueeze(1).to_broadcast([P, S1, E]), ALU.is_ge))
            link(nc.vector.tensor_reduce(es[:, 0, :], ge[:, 0, :, :], X, ALU.add))
            link(nc.vector.tensor_scalar(es[:, 1, :], es[:, 0, :], float(E - 1), None, ALU.min))
            nc.vector.tensor_copy(etab[:, :], es[:, 1, :]).then_inc(s_etab, 1)
            dve.wait_ge(s_ids, 1)
            link(nc.vector.tensor_copy(code_sums[:, :], ps[:, 0, 0:2 * NS]))
            nc.vector.scalar_tensor_tensor(idx[:, :], code_sums[:, 0:NS], float(NOBODY), code_sums[:, NS:], ALU.add,
                                           ALU.add).then_inc(s_idx, 1)
            link(nc.vector.tensor_tensor(ge[:, 1, :, :], es[:, 1, :].unsqueeze(2).to_broadcast([P, S1, E]),
                                         cfs[:, CF["expert"]:CF["expert"] + E].unsqueeze(1).to_broadcast([P, S1, E]),
                                         ALU.is_equal))
            for k, name in ((2, "gam"), (3, "bet")):
                link(nc.vector.tensor_tensor(ge[:, k, :, :], ge[:, 1, :, :],
                                             pbs[:, PB[name]:PB[name] + E].unsqueeze(1).to_broadcast([P, S1, E]),
                                             ALU.mult))
                link(nc.vector.tensor_reduce((gsel if k == 2 else bsel)[:, :], ge[:, k, :, :], X, ALU.add))
            dve.wait_ge(s_bcast, 1)
            nc.vector.engine_nop().then_inc(s_zts, CREDIT)
            nc.vector.engine_nop().then_inc(s_hs, CREDIT)
            nc.vector.engine_nop().then_inc(s_fb, CREDIT)

            def scale_shift(n, par):
                dve.wait_ge(s_zt, n + 1)
                nc.vector.tensor_scalar(zts[:, par, :], ps[:, 6 + par, 0:P], gsel[:, bass.ds(n, 1)],
                                        bsel[:, bass.ds(n, 1)], ALU.mult, ALU.add).then_inc(s_zts, 1)

            def add_bias(n, par, e, later=True):
                dve.wait_ge(s_h, n + 1)
                if later:
                    dve.wait_ge(s_hts, n - 1)
                nc.vector.tensor_tensor(hs[:, par, :].rearrange("p (c n) -> p c n", c=FC),
                                        ps[:, par, :].rearrange("p (c n) -> p c n", c=FC),
                                        b1t[:, bass.ds(e, 1), :].rearrange("p a c -> p (a c)").unsqueeze(2)
                                        .to_broadcast([P, FC, P]), ALU.add).then_inc(s_hs, 1)

            def finish(n, par, e):
                dve.wait_ge(s_f, n + 1 + CREDIT)
                nc.vector.tensor_tensor(fb[:, par, :], ps[:, 4 + par, 0:D],
                                        b2b[:, bass.ds(e, 1), :].rearrange("p a n -> p (a n)"),
                                        ALU.add).then_inc(s_fb, 1)
                dve.wait_ge(s_t2, n + 1)
                dve.wait_ge(s_fb, n + 1 + CREDIT)
                nc.vector.scalar_tensor_tensor(fin[:, bass.ds(n, 1), :].rearrange("p a n -> p (a n)"), fb[:, par, :],
                                               alpha[:, bass.ds(n, 1)],
                                               t2[:, bass.ds(n, 1), :].rearrange("p a n -> p (a n)"),
                                               ALU.mult, ALU.add).then_inc(s_fin, 1)

            regs = [dve.alloc_register(name=f"dve_end{k}") for k in range(2 + NS - TAIL)]
            dve.load(regs[0:2], etab[0:1, 0:2])
            dve.load(regs[2:], etab[0:1, TAIL:NS])
            e_end = [dve.snap(r, min_val=0, max_val=E - 1) for r in regs]
            scale_shift(0, 0)
            for s in range(2):
                scale_shift(s + 1, (s + 1) % 2)
                add_bias(s, s % 2, e_end[s], later=False)
            regs = [dve.alloc_register(name=f"dve_expert{k}") for k in range(LANES + 2)]
            with dve.Fori(0, LOOPS) as i:
                for j in range(LANES):
                    s = i * LANES + 2 + j
                    scale_shift(s + 1, (j + 1) % 2)
                    if j == 0:
                        dve.load(regs, etab[0:1, bass.ds(i * LANES, LANES + 2)])
                        ee = [dve.snap(r, min_val=0, max_val=E - 1) for r in regs]
                    add_bias(s, j % 2, ee[j + 2])
                    finish(i * LANES + j, j % 2, ee[j])
            add_bias(NS - 1, (NS - 1) % 2, e_end[4])
            for n in range(TAIL, NS):
                finish(n, n % 2, e_end[n - TAIL + 2])

        @block.tensor
        def _(pe):
            mm = nc.tensor.matmul

            def keep_clock_up(bank, times):
                for k in range(times):
                    mm(ps[:, bank, :], filler[:, 0:P], filler[:, :], start=True, stop=True)

            pe.wait_ge(s_filler, 1)
            keep_clock_up(1, 8)
            pe.wait_ge(s_pa, 16)
            mm(ps[:, 4, 0:B * KV], pas[:, 0:P], pas[:, PA["ctx"]:PA["ctx"] + B * KV],
               start=True, stop=True).then_inc(s_kt, 1)
            pe.wait_ge(s_ctx4, 1)
            for b in range(B):
                last = mm(ps[:, 5, b * P:(b + 1) * P], ctx4[:, b, :, :].rearrange("p r k -> p (r k)"),
                          pas[:, PA["wv"]:PA["wv"] + P], start=True, stop=True)
            last.then_inc(s_v4p, 1)
            pe.wait_ge(s_cf, 16)
            pe.wait_ge(s_pb, 16)
            mm(ps[:, 0, 0:E], cfs[:, CF["center"]:CF["center"] + P], pbs[:, PB["cen"]:PB["cen"] + E],
               start=True, stop=True).then_inc(s_cent, 1)

            def fold_keys(b):
                pe.wait_ge(s_kblk, b + 1)
                mm(ps[:, 6 + b, :], pas[:, PA["wq"]:PA["wq"] + P], kblk[:, b, :, :].rearrange("p h k -> p (h k)"),
                   start=True, stop=True).then_inc(s_m, 1)

            def turn_x(b):
                pe.wait_ge(s_xn, b + 1)
                for k in range(TB):
                    last = nc.tensor.transpose(ps[:, 2 + b, k * P:(k + 1) * P], xn[:, b * TB + k, :], ident)
                last.then_inc(s_xnt, 1)

            fold_keys(0)
            turn_x(0)
            pe.wait_ge(s_cents, 1)
            mm(ps[:, 1, 0:E], pbs[:, PB["wo"]:PB["wo"] + P], cfs[:, CF["gap"]:CF["gap"] + E],
               start=True, stop=True).then_inc(s_woc, 1)
            fold_keys(1)

            pe.wait_ge(s_cb, 16)
            causal = cbs[0:KV, CB["causal"]:CB["causal"] + P]

            def scores(b, k):
                n = b * TB + k
                bank = ps[:, STOK[n % 3], :]
                pe.wait_ge(s_ms, b + 1)
                pe.wait_ge(s_xnts, b + 1)
                if n == 1:
                    pe.wait_ge(s_wocs, 1)
                if n == 2:
                    pe.wait_ge(s_v4, B)
                if n >= 3:
                    pe.wait_ge(s_max, n - 2)
                last = mm(bank, xnt[:, n * P:(n + 1) * P], ms[:, b, :], start=True, stop=k > 0)
                if k == 0:
                    last = mm(bank.rearrange("p (c n) -> p c n", c=C), identb[0:KV, :],
                              causal.unsqueeze(1).to_broadcast([KV, C, P]), start=False, stop=True)
                last.then_inc(s_stok, 1)

            def shift_cols(b):
                pe.wait_ge(s_split, b + 1)
                for k in range(TB):
                    c0 = b * (T // 2) + k * 64
                    last = nc.tensor.transpose(ps[0:2 * H, 4, c0:c0 + 64].bitcast(BF16),
                                               nm2[:, b, k, :, :].rearrange("p a h -> p (a h)"), identb)
                last.then_inc(s_nmt, 1)

            def scores_t(b, c):
                n = b * C + c
                if n >= 2:
                    pe.wait_ge(s_exp, n - 1)
                pe.wait_ge(s_nmts, b + 1)
                bank = ps[:, 2 + c % 2, :]
                pe.wait_ge(s_low, 2 * (b + 1))
                for k, (m, x) in enumerate(((0, 0), (0, 1), (1, 0))):
                    mm(bank, msr[:, b, m, c * P:(c + 1) * P], xntr[:, b, x, :], start=k == 0, stop=False)
                mm(bank[:, 0:KV], causal, identb[0:KV, 0:KV], start=False, stop=False)
                mm(bank, cbs[0:2 * H, CB["spread"] + c * P:CB["spread"] + (c + 1) * P], nmt[:, b, :],
                   start=False, stop=True).then_inc(s_st, 1)

            def weigh(b, c):
                pe.wait_ge(s_exp, b * C + c + 1)
                for k in range(TB):
                    u = k * C + c
                    last = mm(ps[:, PV[b][u // 8], (u % 8) * 64:(u % 8) * 64 + VW], pt[:, b, c, k * P:(k + 1) * P],
                              v4[:, b, c, :], start=True, stop=True)
                    if c == C - 1 and k % 2 == 1:
                        last.then_inc(s_pv, 1)

            def y_of(b, k):
                return ps[:, (6 if b == 0 else 2) + k // 2, (k % 2) * 256:(k % 2) * 256 + YW]

            def residual(b):
                for k in range(TB):
                    mm(y_of(b, k), xts[:, (b * TB + k) * P:(b * TB + k + 1) * P], identc, start=k % 2 == 0,
                       stop=False, skip_group_check=True)

            def turn_o(b):
                for k in range(TB):
                    if k % 2 == 0:
                        pe.wait_ge(s_o, b * 2 + k // 2 + 1)
                    last = nc.tensor.transpose(ps[:, OT[b][k // 2], k % 2 * P:(k % 2 + 1) * P], o[:, b, k * P:(k + 1) * P], ident)
                    if k % 2 == 1:
                        last.then_inc(s_ot, 1)

            def project(b):
                for k in range(TB):
                    if k % 2 == 0:
                        pe.wait_ge(s_ots, b * 2 + k // 2 + 1)
                    last = mm(y_of(b, k), ot[:, b, k * P:(k + 1) * P], wo_ext, start=False, stop=True,
                              skip_group_check=True)
                    if k % 2 == 1:
                        last.then_inc(s_y, 1)

            before = cbs[:, CB["before"]:CB["before"] + P]
            ones = cbs[:, CB["ones"]:CB["ones"] + P]

            def rank_batch_0():
                pe.wait_ge(s_oh, 1)
                out0 = ps[:, 4, 0:TB * E].rearrange("p (t e) -> p t e", e=E)
                last = mm(out0, before, oh[:, 0:TB, :], start=True, stop=False)
                for t in range(TB - 1):
                    last = mm(out0[:, t + 1:, :], ones, oh[:, t:t + 1, :].to_broadcast([P, TB - 1 - t, E]),
                              start=False, stop=t == TB - 2)
                last.then_inc(s_rank, 1)

            ranks1 = ps[:, 5, 0:(TB + 1) * E].rearrange("p (t e) -> p t e", e=E)

            def seed_ranks():
                pe.wait_ge(s_const, 2)
                for t in range(TB):
                    ins = mm(ranks1, ones, oh[:, t:t + 1, :].to_broadcast([P, TB + 1, E]), start=t == 0, stop=False)
                    if t == 0:
                        ins.then_inc(s_f, CREDIT)

            for k in range(3):
                scores(0, k)
            turn_x(1)
            scores(0, 3)
            scores(1, 0)
            scores(1, 1)
            shift_cols(0)
            scores(1, 2)
            scores(1, 3)
            for c in range(C):
                scores_t(0, c)
            shift_cols(1)
            pe.wait_ge(s_xb, 1)
            pe.wait_ge(s_ms, B)
            residual(0)
            pe.wait_ge(s_vones, 1)
            pe.wait_ge(s_nmts, B)
            for c in range(C):
                scores_t(1, c)
                weigh(0, c)
            weigh(1, 0)
            weigh(1, 1)
            turn_o(0)
            weigh(1, 2)
            weigh(1, 3)
            project(0)
            residual(1)
            turn_o(1)
            project(1)
            rank_batch_0()
            seed_ranks()
            keep_clock_up(1, 6)
            pe.wait_ge(s_oh, B)
            mm(ranks1, before, oh[:, TB:, :], start=False, stop=False)
            for t in range(TB, NT):
                last = mm(ranks1[:, t + 1 - TB:, :], ones, oh[:, t:t + 1, :].to_broadcast([P, NT - t, E]),
                          start=False, stop=t == NT - 1)
            last.then_inc(s_rank, 1)
            keep_clock_up(1, 4)
            pe.wait_ge(s_nmr, B)
            keep_clock_up(1, 5)
            pe.wait_ge(s_row_oh, TB)
            keep_clock_up(1, 3)
            pe.wait_ge(s_row_oh, NT)
            pe.wait_ge(s_tile_oh, 1)
            for t in range(NT):
                last = mm(ps[:, 0, 0:2 * NS], row_oh[:, t, :], tile_code[:, t, :, :].rearrange("p a s -> p (a s)"),
                          start=t == 0, stop=t == NT - 1)
            last.then_inc(s_ids, 1)
            keep_clock_up(1, 14)

            def turn(n, par, lane, seen):
                pe.wait_ge(s_zl[lane], seen * 16 + 16)
                pe.wait_ge(s_zts, n + 1)
                nc.tensor.transpose(ps[:, 6 + par, 0:P], zl[:, lane, 0:D], ident).then_inc(s_zt, 1)

            def first(n, par):
                pe.wait_ge(s_w1c, n + 1)
                pe.wait_ge(s_zts, n + 1 + CREDIT)
                pe.wait_ge(s_hs, n + 1)
                for c in range(FC):
                    last = mm(ps[:, par, c * P:(c + 1) * P], w1c[:, par, c * P:(c + 1) * P], zts[:, par, :],
                              start=True, stop=True)
                last.then_inc(s_h, 1)

            def second(n, par, e):
                pe.wait_ge(s_hts, n + 1)
                pe.wait_ge(s_fb, n + 1)
                for c in range(FC):
                    last = mm(ps[:, 4 + par, 0:D], hts[:, par, c * P:(c + 1) * P],
                              w2s[:, bass.ds(e, 1), c * D:(c + 1) * D].rearrange("p a n -> p (a n)"),
                              start=c == 0, stop=c == FC - 1)
                last.then_inc(s_f, 1)

            pe.wait_ge(s_etab, 1)
            pe.wait_ge(s_w2, 16)
            regs = [pe.alloc_register(name=f"pe_end{k}") for k in range(NS - TAIL)]
            pe.load(regs, etab[0:1, TAIL:NS])
            e_end = [pe.snap(r, min_val=0, max_val=E - 1) for r in regs]
            turn(0, 0, 0, 0)
            turn(1, 1, 1, 0)
            first(0, 0)
            turn(2, 0, 2, 0)
            first(1, 1)
            regs = [pe.alloc_register(name=f"pe_expert{k}") for k in range(LANES)]
            with pe.Fori(0, LOOPS) as i:
                for j in range(LANES):
                    s = i * LANES + 2 + j
                    turn(s + 1, (j + 1) % 2, (3 + j) % LANES, i + (3 + j) // LANES)
                    first(s, j % 2)
                    if j == 0:
                        pe.load(regs, etab[0:1, bass.ds(i * LANES, LANES)])
                        ee = [pe.snap(r, min_val=0, max_val=E - 1) for r in regs]
                    second(s - 2, j % 2, ee[j])
            first(NS - 1, 0)
            for n in range(TAIL, NS):
                second(n, n % 2, e_end[n - TAIL])


def constants():
    import numpy as np
    cf = np.zeros((P, CF_W), np.float32)
    r = np.arange(P)
    cf[:, CF["ident"]:CF["ident"] + P] = np.eye(P)
    cf[:, CF["center"]:CF["center"] + P] = np.eye(P) - 1.0 / D
    cf[:, CF["hmask"]:CF["hmask"] + H] = r[:, None] // HD == np.arange(H)[None]
    cf[:, CF["vmask"]:CF["vmask"] + HC * HD] = r[:, None] // KV == np.arange(HC * HD)[None] // HD
    cf[:, CF["ones"]:CF["ones"] + HC] = r[:, None] // KV == np.arange(HC)[None]
    cf[:, CF["desc"]:CF["desc"] + E] = E - np.arange(E)[None]
    cf[:, CF["code"]:CF["code"] + NT] = P * np.arange(NT)[None] - NOBODY
    cf[:, CF["row"]] = r
    cf[:, CF["expert"]:CF["expert"] + E] = np.arange(E)[None]
    cf[:, CF["slot"]:CF["slot"] + NS + 1] = P * np.arange(NS + 1)[None]
    cb = np.zeros((P, CB_W), np.float32)
    cb[:, CB["ident"]:CB["ident"] + P] = np.eye(P)
    cb[:, CB["before"]:CB["before"] + P] = r[:, None] < r[None]
    cb[:, CB["ones"]:CB["ones"] + P] = 1.0
    rows = np.arange(2 * H)[:, None] % H
    cb[0:2 * H, CB["spread"]:CB["spread"] + C * P] = rows == np.arange(C * P)[None] // KV
    cb[0:KV, CB["causal"]:CB["causal"] + P] = np.where(np.arange(P)[None] % KV > np.arange(KV)[:, None], NEG, 0.0)
    cb[:, CB["lane"]:CB["lane"] + P] = r[None]
    return cf, (cb.view(np.uint32) >> 16).astype(np.uint16)


def kernel(x, ctx_1024, L0_xattn_Wq, L0_xattn_Wk, L0_xattn_Wv, L0_xattn_Wo, L0_xattn_bo, L0_ffn_centroids,
           L0_ffn_gamma, L0_ffn_beta, L0_ffn_W1, L0_ffn_b1, L0_ffn_W2, L0_ffn_b2):
    import numpy as np
    import concourse.bacc as bacc
    from concourse import mybir as mb
    from concourse.bass_utils import run_bass_kernel_spmd as run

    def a(v):
        return np.asarray(v)
    cf, cb = constants()
    arrays = {
        "x": np.ascontiguousarray(a(x)),
        "xt": np.ascontiguousarray(a(x).reshape(B * T, D).T),
        "pa": np.ascontiguousarray(np.concatenate([
            a(L0_xattn_Wk).T, a(ctx_1024).reshape(B * KV, D).T, a(L0_xattn_Wv).T, a(L0_xattn_Wq)], axis=1)),
        "pb": np.ascontiguousarray(np.concatenate([
            a(L0_xattn_Wo), a(L0_xattn_Wo).T, a(L0_ffn_centroids).T, a(L0_ffn_gamma).T, a(L0_ffn_beta).T,
            a(L0_ffn_b1).reshape(E * FC, P).T, a(L0_xattn_bo)[:, None]], axis=1)),
        "cf": cf,
        "cb": cb,
        "b2": np.ascontiguousarray(a(L0_ffn_b2).reshape(1, -1)),
        "w1": np.ascontiguousarray(a(L0_ffn_W1).transpose(2, 0, 1)),
        "w2": np.ascontiguousarray(a(L0_ffn_W2).reshape(E, D, FC, P).transpose(3, 0, 2, 1).reshape(P, E, FC * D)),
    }
    nc = bacc.Bacc("TRN2", target_bir_lowering=False, num_devices=1)
    aps = [nc.dram_tensor(f"in_{k}", v.shape, mb.dt.from_np(v.dtype), kind="ExternalInput").ap()
           for k, v in arrays.items()]
    out = nc.dram_tensor("out", (B, T, D), mb.dt.float32, kind="ExternalOutput").ap()
    xattn_moe(nc, *aps, out)
    r = run(nc, [{f"in_{k}": v for k, v in arrays.items()}], core_ids=[0])
    return r.results[0]["out"]
```
